# Optimizing a Trainium2 kernel written in Bass

```python
import numpy as np
import jax
import jax.numpy as jnp

def _softmax(x, axis=-1):
    return jax.nn.softmax(x, axis=axis)

def _gelu(x):
    return jax.nn.gelu(x, approximate=True)

def _silu(x):
    return jax.nn.silu(x)

def _sigmoid(x):
    return jax.nn.sigmoid(x)

def _layernorm(x, axis=-1, eps=1e-05):
    m = jnp.mean(x, axis=axis, keepdims=True)
    v = jnp.var(x, axis=axis, keepdims=True)
    return (x - m) / jnp.sqrt(v + eps)

def _scatter_add(tgt, idx, src, axis=0):
    return tgt.at[idx].add(src)

def _segment_sum(src, seg, n):
    return jax.ops.segment_sum(src, seg, n)
kernel_name = 'mk_gnn_preln_d1_gnn_r8_c50dc4'

def setup_inputs(seed: int=0):
    np.random.seed(seed)
    _w = jnp.asarray

    def _rec_inputs():
        import jax
        import jax.numpy as jnp
        _gk = jax.random.key(seed)
        x = -0.0003713 + 1 * jax.random.normal(jax.random.fold_in(_gk, 1), (6250, 256), jnp.float32)
        _s = jax.random.randint(jax.random.fold_in(_gk, 2), (100000,), 0, 6250, jnp.int32)
        _d = jax.random.randint(jax.random.fold_in(_gk, 3), (100000,), 0, 6250, jnp.int32)
        _loop = jnp.arange(6250, dtype=jnp.int32)
        src = jnp.concatenate([_s, _d, _loop])
        dst = jnp.concatenate([_d, _s, _loop])
        _o = jnp.argsort(dst, stable=True)
        src = src[_o]
        dst = dst[_o]
        edge_attr_128 = -5.16925e-05 + 1.00005 * jax.random.normal(jax.random.fold_in(_gk, 11), (206250, 128), jnp.float32)
        return (x, src, dst, edge_attr_128)
    x, src, dst, edge_attr_128 = _rec_inputs()

    def _L0_gnn_setup():
        import jax, jax.numpy as jnp
        import numpy as np
        N_NODES = 6250
        N_EDGES = 100000
        IN_DIM = 256
        OUT_DIM = 256
        HEADS = 1
        EDGE_DIM = 128
        NEG_SLOPE = 0.01
        key = jax.random.key(seed)
        ks = jax.random.split(key, 8)
        x = jax.random.normal(ks[0], (N_NODES, IN_DIM), dtype=jnp.float32)
        edge_index = jax.random.randint(ks[1], (2, N_EDGES), 0, N_NODES, dtype=jnp.int64)
        edge_attr = jax.random.normal(ks[2], (N_EDGES, EDGE_DIM), dtype=jnp.float32)
        hc = HEADS * OUT_DIM
        Wn = jax.random.normal(ks[3], (hc, IN_DIM), dtype=jnp.float32) / np.sqrt(IN_DIM)
        bn = jnp.zeros((hc,), dtype=jnp.float32)
        We = jax.random.normal(ks[4], (hc, EDGE_DIM), dtype=jnp.float32) / np.sqrt(EDGE_DIM)
        be = jnp.zeros((hc,), dtype=jnp.float32)
        attn = jax.random.normal(ks[5], (1, HEADS, OUT_DIM), dtype=jnp.float32) * np.sqrt(2.0 / (HEADS * OUT_DIM + 1))
        return {'x': x, 'edge_index': edge_index, 'edge_attr': edge_attr, 'Wn': Wn, 'bn': bn, 'We': We, 'be': be, 'attn': attn}
    _L0_gnn_all = _L0_gnn_setup()
    _L0_gnn_in = {k: v for k, v in _L0_gnn_all.items() if k in ('Wn', 'bn', 'We', 'be', 'attn')}
    del _L0_gnn_all
    return {'x': x, 'src': src, 'dst': dst, 'edge_attr_128': edge_attr_128, 'L0_gnn_Wn': _L0_gnn_in['Wn'], 'L0_gnn_bn': _L0_gnn_in['bn'], 'L0_gnn_We': _L0_gnn_in['We'], 'L0_gnn_be': _L0_gnn_in['be'], 'L0_gnn_attn': _L0_gnn_in['attn']}

def reference(x, src, dst, edge_attr_128, L0_gnn_Wn, L0_gnn_bn, L0_gnn_We, L0_gnn_be, L0_gnn_attn):
    import jax
    import jax.numpy as jnp

    def _L0_gnn_ref(x, edge_index, edge_attr, Wn, bn, We, be, attn):
        import jax, jax.numpy as jnp
        import numpy as np
        N_NODES = 6250
        N_EDGES = 100000
        IN_DIM = 256
        OUT_DIM = 256
        HEADS = 1
        EDGE_DIM = 128
        NEG_SLOPE = 0.01
        N = x.shape[0]
        H, C = (attn.shape[1], attn.shape[2])
        src, dst = (edge_index[0], edge_index[1])
        h = x @ Wn.T + bn
        e = edge_attr @ We.T + be
        xj = h[src].reshape(-1, H, C)
        ee = e.reshape(-1, H, C)
        a = jax.nn.leaky_relu(jnp.sum((xj + ee) * attn, axis=-1), NEG_SLOPE)
        m = jax.ops.segment_max(a, dst, num_segments=N)
        a = jnp.exp(a - m[dst])
        denom = jax.ops.segment_sum(a, dst, num_segments=N)
        a = a / (denom[dst] + 1e-16)
        msg = (xj * a[..., None]).reshape(-1, H * C)
        out = jax.ops.segment_sum(msg, dst, num_segments=N)
        return jax.nn.relu(out)
    edge_index = jnp.stack([src, dst])
    h = jnp.maximum(_layernorm(x, axis=-1), 0.0)
    x = x + _L0_gnn_ref(h, edge_index, edge_attr_128, L0_gnn_Wn, L0_gnn_bn, L0_gnn_We, L0_gnn_be, L0_gnn_attn)
    return x

_drawn_inputs = setup_inputs


def setup_inputs(seed=0):
    import zlib

    import numpy as np

    out = dict(_drawn_inputs(seed))
    spreads = {'L0_gnn_bn': (0.0, 0.1), 'L0_gnn_be': (0.0, 2.0)}
    factors = {}
    for name, (base, spread) in spreads.items():
        noise = np.random.default_rng([zlib.crc32(name.encode()), seed]).standard_normal(out[name].shape)
        drawn = base * np.exp(spread * noise) if base else spread * noise
        out[name] = jnp.asarray(drawn.astype(out[name].dtype))
    for name, factor in factors.items():
        out[name] = (out[name] * factor).astype(out[name].dtype)
    return out
```

```python
from contextlib import ExitStack

import concourse.bass as bass
from concourse import mybir

ALU = mybir.AluOpType
ACT = mybir.ActivationFunctionType
AX = mybir.AxisListType
F32 = mybir.dt.float32
I32 = mybir.dt.int32

P = 128
TILES = 12
SLOTS = 3
WINDOW = 64
CHUNK = TILES * P
NODES_PER_ROW = 7
ROW_PAD = 8
NEG_SLOPE = 0.01
LN_EPS = 1e-5
DENOM_EPS = 1e-16
MASKED = -(2.0 ** 100)
NO_MAX = -(2.0 ** 90)


def chunks_of(n_edges):
    n = -(-n_edges // CHUNK)
    return -(-n // SLOTS) * SLOTS


def chunk_start(c, n_edges):
    return min(c * CHUNK, n_edges - CHUNK)


def gnn_layer(nc, x, src_slots, dst_slots, edge_attr, Wn, WnT, We, bn, vectors, out):
    N, D = x.shape
    E, DE = edge_attr.shape
    ROW = D + ROW_PAD
    NCH = chunks_of(E)
    FULL = E // CHUNK
    GROUPS = NCH // SLOTS
    H = D // P
    GROUP_NODES = NODES_PER_ROW * P
    TABLE_GROUPS = -(-N // GROUP_NODES)
    BLOCKS = -(-N // P)
    WINDOWS = -(-N // WINDOW)
    NODE_COLS = BLOCKS * P + WINDOW
    SEL_EDGES = NCH * TILES
    assert D == 2 * P and DE == P and N >= GROUP_NODES and E >= CHUNK and NCH <= 512

    table = nc.dram_tensor("row_table", [N, ROW], F32, kind="Internal").ap()

    with ExitStack() as ctx:
        def sb(name, shape, dt=F32):
            return ctx.enter_context(nc.sbuf_tensor(name, shape, dt))

        def slots(stack, name, shape):
            return [stack.enter_context(nc.sbuf_tensor(f"{name}{s}", shape, F32)) for s in range(SLOTS)]

        def ps(name, shape):
            return ctx.enter_context(nc.psum_tensor(name, shape, F32))

        def sem(name):
            return ctx.enter_context(nc.semaphore(name))

        ident = sb("ident", [P, P])
        ones = sb("ones", [P, P])
        last_row = sb("last_row", [P, P])
        first_row = sb("first_row", [P, 1])
        node_iota = sb("node_iota", [P, WINDOW])
        wn_sb = sb("wn_sb", [P, H, D])
        wnT_sb = sb("wnT_sb", [P, H, D])
        we_sb = sb("we_sb", [P, H, DE])
        cols = sb("cols", [P, 3, H])
        bn_rows = sb("bn_rows", [P, D])
        attn_wide = sb("attn_wide", [P, H, P])
        u_bc = sb("u_bc", [P, D])
        v_bc = sb("v_bc", [P, DE])
        score_const = sb("score_const", [P, 2])
        dst_i = sb("dst_i", [P, SEL_EDGES], I32)
        dst_loc = sb("dst_loc", [P, SEL_EDGES])
        base_bc = sb("base_bc", [P, NCH])
        base_i = sb("base_i", [P, NCH], I32)
        src_idx = sb("src_idx", [P, SLOTS, TILES], I32)
        node_max = sb("node_max", [P, NODE_COLS])
        sums = sb("sums", [P, H + 1, NODE_COLS])
        tile_max = sb("tile_max", [P, P])
        outside_i = sb("outside_i", [P, 1], I32)
        dst_left = sb("dst_left", [P, TILES])
        below_end = sb("below_end", [P, TILES])
        in_window = sb("in_window", [P, TILES])

        t_maxT = ps("t_maxT", [P, P])
        t_maxB = ps("t_maxB", [P, WINDOW])
        t_sums = [ps(f"t_sums{s}", [P, H + 1, WINDOW]) for s in range(SLOTS)]
        t_out = [ps(f"t_out{s}", [P, 512]) for s in range(SLOTS)]

        t_setup = [t_out[0], t_out[1]]

        weights_in = sem("weights_in")
        dst_in = sem("dst_in")
        consts_ready = sem("consts_ready")
        ident_ready = sem("ident_ready")
        state_ready = sem("state_ready")
        src_in = [sem(f"src_in{s}") for s in range(SLOTS)]
        attr_in = [sem(f"attr_in{s}") for s in range(SLOTS)]
        rows_in = [sem(f"rows_in{s}") for s in range(SLOTS)]
        setup_step = sem("setup_step")
        attn_ready = sem("attn_ready")
        spread_ready = sem("spread_ready")
        vectors_ready = sem("vectors_ready")
        dst_float = sem("dst_float")
        base_spread = sem("base_spread")
        x_in = [sem(f"x_in{s}") for s in range(2)]
        stats_ready = sem("stats_ready")
        norm_step = sem("norm_step")
        var_ready = sem("var_ready")
        dev_ready = sem("dev_ready")
        norm_ready = sem("norm_ready")
        normed = sem("normed")
        row_ready = sem("row_ready")
        table_out = [sem(f"table_out{s}") for s in range(2)]
        attr_used = sem("attr_used")
        summed = sem("summed")
        scored = sem("scored")
        differs = sem("differs")
        masked_ready = sem("masked_ready")
        tile_max_ready = sem("tile_max_ready")
        maxT_ready = sem("maxT_ready")
        chunk_max_ready = sem("chunk_max_ready")
        diag_ready = sem("diag_ready")
        maxB_ready = sem("maxB_ready")
        new_max_ready = sem("new_max_ready")
        drop_ready = sem("drop_ready")
        max_stored = sem("max_stored")
        shifted = sem("shifted")
        decay_ready = sem("decay_ready")
        weights_ready = sem("weights_ready")
        sums_ready = sem("sums_ready")
        decayed = sem("decayed")
        sums_added = sem("sums_added")
        counted = sem("counted")
        count_spread = sem("count_spread")
        outside_ready = sem("outside_ready")
        left_step = sem("left_step")
        left_moved = sem("left_moved")
        passed = sem("passed")

        def stand(eng):
            eng.sem_inc(passed, 1)

        def per_tile(ap):
            return ap.unsqueeze(2).to_broadcast([P, TILES, WINDOW])

        def per_node(ap):
            return ap.unsqueeze(1).to_broadcast([P, TILES, WINDOW])

        def has(c, n):
            return not isinstance(c, int) or c >= n

        with ExitStack() as st:
            x_rows = [st.enter_context(nc.sbuf_tensor(f"x_rows{s}", [P, NODES_PER_ROW, D], F32)) for s in range(2)]
            t_rows = [st.enter_context(nc.sbuf_tensor(f"t_rows{s}", [P, NODES_PER_ROW, ROW], F32)) for s in range(2)]
            stats = [st.enter_context(nc.sbuf_tensor(f"stats{s}", [P, NODES_PER_ROW, 6], F32)) for s in range(2)]
            mean_var = [st.enter_context(nc.sbuf_tensor(f"mean_var{s}", [P, NODES_PER_ROW, 2], F32)) for s in range(2)]
            var_eps = [st.enter_context(nc.sbuf_tensor(f"var_eps{s}", [P, NODES_PER_ROW], F32)) for s in range(2)]
            dev = [st.enter_context(nc.sbuf_tensor(f"dev{s}", [P, NODES_PER_ROW], F32)) for s in range(2)]
            rstd = [st.enter_context(nc.sbuf_tensor(f"rstd{s}", [P, NODES_PER_ROW], F32)) for s in range(2)]
            shift = [st.enter_context(nc.sbuf_tensor(f"shift{s}", [P, NODES_PER_ROW], F32)) for s in range(2)]
            scrap = st.enter_context(nc.sbuf_tensor("scrap", [P, NODES_PER_ROW, D], F32))

            def node_group(ap, q):
                at = min(q * GROUP_NODES, N - GROUP_NODES)
                return ap[at:at + GROUP_NODES, :].rearrange("(p r) c -> p r c", r=NODES_PER_ROW)

            block = st.enter_context(nc.Block())

            @block.sync
            def _(sp):
                for q in range(TABLE_GROUPS):
                    if q >= 2:
                        sp.wait_ge(row_ready, q - 1)
                    sp.dma_start(x_rows[q % 2][:], node_group(x, q)).then_inc(x_in[q % 2], 16)
                    if q == 0:
                        sp.dma_start(cols[:], vectors).then_inc(weights_in, 16)
                        sp.dma_start(wn_sb[:], Wn.rearrange("(h p) i -> p h i", p=P)).then_inc(weights_in, 16)
                        sp.dma_start(we_sb[:], We.rearrange("(h p) i -> p h i", p=P)).then_inc(weights_in, 16)
                        sp.dma_start(dst_i[:], dst_slots).then_inc(dst_in, 16)
                        sp.dma_start(wnT_sb[:], WnT.rearrange("(h p) o -> p h o", p=P)).then_inc(dst_in, 16)
                        sp.wait_ge(state_ready, 1)
                        sp.dma_start(bn_rows[0:1, :], bn.rearrange("(a d) -> a d", a=1)).then_inc(dst_in, 16)

            @block.gpsimd
            def _(pool):
                nc.gpsimd.memset(ones[:], 1.0)
                nc.gpsimd.memset(ident[:], 0.0)
                nc.gpsimd.memset(last_row[:], 0.0)
                nc.gpsimd.memset(first_row[:], 0.0)
                nc.gpsimd.memset(tile_max[:], 0.0)
                for s in range(2):
                    nc.gpsimd.memset(t_rows[s][:, :, D:ROW], 0.0)
                nc.gpsimd.iota(node_iota[:], pattern=[[1, WINDOW]], base=0, channel_multiplier=0,
                               allow_small_or_imprecise_dtypes=True)
                nc.gpsimd.memset(bn_rows[:], 0.0).then_inc(state_ready, 1)
                pool.wait_ge(state_ready, 1)
                nc.gpsimd.affine_select(out=ident[:], in_=ident[:], compare_op=ALU.not_equal, fill=1.0,
                                        base=0, pattern=[[-1, P]], channel_multiplier=1)
                nc.gpsimd.affine_select(out=last_row[:], in_=last_row[:], compare_op=ALU.not_equal, fill=1.0,
                                        base=-(P - 1), pattern=[[0, P]], channel_multiplier=1)
                nc.gpsimd.affine_select(out=first_row[:], in_=first_row[:], compare_op=ALU.not_equal, fill=1.0,
                                        base=0, pattern=[[0, 1]], channel_multiplier=1).then_inc(consts_ready, 1)
                nc.gpsimd.memset(node_max[:], NO_MAX)
                nc.gpsimd.memset(sums[:], 0.0).then_inc(state_ready, 1)

            @block.tensor
            def _(pe):
                pe.wait_ge(consts_ready, 1)
                pe.wait_ge(weights_in, 3 * 16)
                pe.wait_ge(attn_ready, 1)
                for h in range(H):
                    pe.matmul(t_setup[0][:, 0:D], attn_wide[:, h, :], wn_sb[:, h, :], start=(h == 0), stop=(h == H - 1))
                for h in range(H):
                    pe.matmul(t_setup[0][:, D:D + DE], attn_wide[:, h, :], we_sb[:, h, :], start=(h == 0), stop=(h == H - 1))
                for h in range(H):
                    mm = pe.matmul(t_setup[0][:, D + DE:D + DE + 2], attn_wide[:, h, :], cols[:, 1:3, h],
                                   start=(h == 0), stop=(h == H - 1))
                mm.then_inc(spread_ready, 1)
                pe.wait_ge(dst_float, 1)
                pe.matmul(t_setup[1][:, 0:NCH], last_row[:],
                          dst_loc[:].rearrange("p (c j) -> p c j", j=TILES)[:, :, TILES - 1],
                          start=True, stop=True).then_inc(base_spread, 1)

            def stats_of(dve, q):
                s = q % 2
                dve.wait_ge(x_in[s], 16 * (q // 2 + 1))
                for r in range(NODES_PER_ROW):
                    last = nc.vector.bn_stats(stats[s][:, r, :], x_rows[s][:, r, :])
                last.then_inc(stats_ready, 1)
                dve.wait_ge(stats_ready, q + 1)
                for r in range(NODES_PER_ROW):
                    last = nc.vector.bn_aggr(mean_var[s][:, r, :], stats[s][:, r, :])
                last.then_inc(norm_step, 1)
                dve.wait_ge(norm_step, 2 * q + 1)
                if q >= 2:
                    dve.wait_ge(normed, q - 1)
                nc.vector.tensor_scalar(var_eps[s][:], mean_var[s][:, :, 1], LN_EPS, None, ALU.add).then_inc(var_ready, 1)

            def shift_of(dve, q):
                s = q % 2
                dve.wait_ge(dev_ready, q + 1)
                nc.vector.reciprocal(rstd[s][:], dev[s][:]).then_inc(norm_step, 1)
                dve.wait_ge(norm_step, 2 * q + 2)
                nc.vector.scalar_tensor_tensor(shift[s][:], mean_var[s][:, :, 0], -1.0, rstd[s][:],
                                               ALU.mult, ALU.mult).then_inc(norm_ready, 1)

            def node_scores(dve, q):
                s = q % 2
                dve.wait_ge(normed, q + 1)
                if q >= 1:
                    dve.wait_ge(row_ready, q)
                for r in range(NODES_PER_ROW):
                    last = nc.vector.tensor_tensor_reduce(scrap[:, r, :], t_rows[s][:, r, 0:D], u_bc[:], 1.0,
                                                          score_const[:, 0:1], ALU.mult, ALU.add,
                                                          t_rows[s][:, r, D:D + 1])
                last.then_inc(row_ready, 1)

            @block.vector
            def _(dve):
                dve.wait_ge(consts_ready, 1)
                dve.wait_ge(weights_in, 3 * 16)
                for h in range(H):
                    last = nc.vector.tensor_scalar(attn_wide[:, h, :], ones[:], cols[:, 0, h:h + 1], None, ALU.mult)
                last.then_inc(attn_ready, 1)
                stats_of(dve, 0)
                shift_of(dve, 0)
                dve.wait_ge(spread_ready, 1)
                nc.vector.tensor_copy(u_bc[:], t_setup[0][:, 0:D])
                nc.vector.tensor_copy(v_bc[:], t_setup[0][:, D:D + DE])
                nc.vector.tensor_copy(score_const[:], t_setup[0][:, D + DE:D + DE + 2]).then_inc(setup_step, 1)
                dve.wait_ge(setup_step, 1)
                nc.vector.tensor_tensor(score_const[:, 0:1], score_const[:, 0:1], score_const[:, 1:2],
                                        ALU.add).then_inc(vectors_ready, 1)
                dve.wait_ge(vectors_ready, 1)
                for q in range(TABLE_GROUPS):
                    if q + 1 < TABLE_GROUPS:
                        stats_of(dve, q + 1)
                    node_scores(dve, q)
                    if q + 1 < TABLE_GROUPS:
                        shift_of(dve, q + 1)
                dve.wait_ge(dst_in, 3 * 16)
                nc.vector.tensor_copy(dst_loc[:], dst_i[:]).then_inc(dst_float, 1)
                dve.wait_ge(base_spread, 1)
                nc.vector.tensor_scalar(base_bc[:], t_setup[1][:, 0:NCH], float(WINDOW - 1), 0.0,
                                        ALU.subtract, ALU.max).then_inc(setup_step, 1)
                dve.wait_ge(setup_step, 2)
                nc.vector.tensor_copy(base_i[:], base_bc[:])
                dst_by_chunk = dst_loc[:].rearrange("p (c j) -> p c j", j=TILES)
                nc.vector.tensor_tensor(dst_by_chunk, dst_by_chunk,
                                        base_bc[:].unsqueeze(2).to_broadcast([P, NCH, TILES]),
                                        ALU.subtract).then_inc(setup_step, 1)
                dve.wait_ge(setup_step, 3)

            def store(act, q):
                act.wait_ge(row_ready, q + 1)
                if q == TABLE_GROUPS - 1:
                    act.wait_ge(table_out[(q - 1) % 2], 16 * ((q - 1) // 2 + 1))
                act.dma_start(node_group(table, q), t_rows[q % 2][:]).then_inc(table_out[q % 2], 16)

            @block.scalar
            def _(act):
                def deviation(q):
                    act.wait_ge(var_ready, q + 1)
                    nc.scalar.activation(dev[q % 2][:], var_eps[q % 2][:], ACT.Sqrt).then_inc(dev_ready, 1)

                deviation(0)
                for q in range(TABLE_GROUPS):
                    s = q % 2
                    act.wait_ge(norm_ready, q + 1)
                    if q == 0:
                        act.wait_ge(consts_ready, 1)
                    if q >= 2:
                        act.wait_ge(table_out[s], 16 * (q // 2))
                    for r in range(NODES_PER_ROW):
                        last = nc.scalar.activation(t_rows[s][:, r, 0:D], x_rows[s][:, r, :], ACT.Relu,
                                                    bias=shift[s][:, r:r + 1], scale=rstd[s][:, r:r + 1])
                    last.then_inc(normed, 1)
                    if q + 1 < TABLE_GROUPS:
                        deviation(q + 1)
                    if q >= 1:
                        store(act, q - 1)
                store(act, TABLE_GROUPS - 1)
                for s in range(2):
                    act.wait_ge(table_out[s], 16 * ((TABLE_GROUPS + 1 - s) // 2))

        chunk_stack = ctx.enter_context(ExitStack())

        def chunk_sb(name, shape, dt=F32):
            return chunk_stack.enter_context(nc.sbuf_tensor(name, shape, dt))

        rows = chunk_sb("rows", [P, SLOTS, TILES, ROW])
        attr = chunk_sb("attr", [P, SLOTS, TILES, DE])
        attr_dot = chunk_sb("attr_dot", [P, TILES])
        score_sum = chunk_sb("score_sum", [P, TILES])
        score = chunk_sb("score", [P, TILES])
        masked = chunk_sb("masked", [P, TILES, WINDOW])
        weights = chunk_sb("weights", [P, SLOTS, TILES, WINDOW])
        chunk_max = chunk_sb("chunk_max", [WINDOW, 1])
        max_diag = chunk_sb("max_diag", [WINDOW, WINDOW])
        new_max = chunk_sb("new_max", [P, WINDOW])
        max_drop = chunk_sb("max_drop", [P, SLOTS, WINDOW])
        decay = chunk_sb("decay", [P, SLOTS, WINDOW])
        in_flag = chunk_sb("in_flag", [P, SEL_EDGES])
        in_count = chunk_sb("in_count", [P, 1])

        def dot_attr(dve, s, landed, tiles):
            if tiles[0] == 0:
                dve.wait_ge(attr_in[s], landed)
            for j in tiles:
                last = nc.vector.tensor_tensor_reduce(attr[:, s, j, :], attr[:, s, j, :], v_bc[:], 1.0, 0.0,
                                                      ALU.mult, ALU.add, attr_dot[:, j:j + 1])
            if tiles[-1] == TILES - 1:
                last.then_inc(attr_used, 1)

        def add_scores(dve, s, c, landed):
            dve.wait_ge(rows_in[s], landed)
            dve.wait_ge(attr_used, c + 1)
            nc.vector.tensor_tensor(score_sum[:], attr_dot[:], rows[:, s, :, D], ALU.add).then_inc(summed, 1)
            dve.wait_ge(summed, c + 1)
            nc.vector.scalar_tensor_tensor(score[:], score_sum[:], NEG_SLOPE, score_sum[:],
                                           ALU.mult, ALU.max).then_inc(scored, 1)

        def compare(dve, c, dst_here):
            nc.vector.tensor_tensor(masked[:], per_node(node_iota[:]), per_tile(dst_here),
                                    ALU.not_equal).then_inc(differs, 1)

        def mask(dve, c, chunks):
            dve.wait_ge(differs, c + 1)
            dve.wait_ge(scored, chunks + 1)
            nc.vector.scalar_tensor_tensor(masked[:], masked[:], MASKED, per_tile(score[:]),
                                           ALU.mult, ALU.add).then_inc(masked_ready, 1)
            dve.wait_ge(masked_ready, c + 1)
            if has(c, 1):
                dve.wait_ge(maxT_ready, c)
            nc.vector.tensor_reduce(tile_max[:, 0:WINDOW], masked[:].rearrange("p j n -> p n j"),
                                    AX.X, ALU.max).then_inc(tile_max_ready, 1)

        def chunk_maximum(dve, c):
            dve.wait_ge(maxT_ready, c + 1)
            nc.vector.tensor_reduce(chunk_max[:], t_maxT[0:WINDOW, :], AX.X, ALU.max).then_inc(chunk_max_ready, 1)
            dve.wait_ge(chunk_max_ready, c + 1)
            if has(c, 1):
                dve.wait_ge(maxB_ready, c)
            nc.vector.tensor_scalar(max_diag[:], ident[0:WINDOW, 0:WINDOW], chunk_max[:, 0:1], None,
                                    ALU.mult).then_inc(diag_ready, 1)

        def grow_maximum(dve, c, s, first_node):
            here = node_max[:, bass.ds(first_node, WINDOW)]
            dve.wait_ge(maxB_ready, c + 1)
            nc.vector.tensor_tensor(new_max[:], here, t_maxB[:], ALU.max).then_inc(new_max_ready, 1)
            dve.wait_ge(new_max_ready, c + 1)
            if has(c, SLOTS):
                dve.wait_ge(decay_ready, c - SLOTS + 1)
            nc.vector.tensor_tensor(max_drop[:, s, :], here, new_max[:], ALU.subtract).then_inc(drop_ready, 1)
            nc.vector.tensor_tensor(masked[:], masked[:], per_node(new_max[:]), ALU.subtract).then_inc(shifted, 1)
            dve.wait_ge(drop_ready, c + 1)
            nc.vector.tensor_tensor(here, new_max[:], new_max[:], ALU.max).then_inc(max_stored, 1)

        def add_sums(dve, c, s, first_node):
            here = sums[:, :, bass.ds(first_node, WINDOW)]
            dve.wait_ge(decay_ready, c + 1)
            if has(c, 1):
                dve.wait_ge(sums_added, c)
            nc.vector.tensor_tensor(here, here, decay[:, s, :].unsqueeze(1).to_broadcast([P, H + 1, WINDOW]),
                                    ALU.mult).then_inc(decayed, 1)
            dve.wait_ge(decayed, c + 1)
            dve.wait_ge(sums_ready, c + 1)
            nc.vector.tensor_tensor(here, here, t_sums[s][:], ALU.add).then_inc(sums_added, 1)

        def products(pe, c, s):
            pe.wait_ge(tile_max_ready, c + 1)
            if has(c, 1):
                pe.wait_ge(chunk_max_ready, c)
            pe.transpose(t_maxT[:], tile_max[:], ident[:]).then_inc(maxT_ready, 1)
            pe.wait_ge(diag_ready, c + 1)
            if has(c, 1):
                pe.wait_ge(new_max_ready, c)
            pe.matmul(t_maxB[:], ones[0:WINDOW, :], max_diag[:], start=True, stop=True).then_inc(maxB_ready, 1)
            pe.wait_ge(weights_ready, c + 1)
            if has(c, SLOTS):
                pe.wait_ge(sums_added, c - SLOTS + 1)
            for h in range(H + 1):
                for j in range(TILES):
                    mm = pe.matmul(t_sums[s][:, h, :], rows[:, s, j, h * P:(h + 1) * P] if h < H else ones[:],
                                   weights[:, s, j, :], start=(j == 0), stop=(j == TILES - 1))
            mm.then_inc(sums_ready, 1)

        def exponentials(act, c, s):
            act.wait_ge(drop_ready, c + 1)
            if has(c, SLOTS):
                act.wait_ge(decayed, c - SLOTS + 1)
                act.wait_ge(sums_ready, c - SLOTS + 1)
            nc.scalar.activation(decay[:, s, :], max_drop[:, s, :], ACT.Exp).then_inc(decay_ready, 1)
            act.wait_ge(shifted, c + 1)
            nc.scalar.activation(weights[:, s, :, :], masked[:], ACT.Exp).then_inc(weights_ready, 1)

        with ExitStack() as st:
            block = st.enter_context(nc.Block())

            @block.sync
            def _(sp):
                def load(c, g, s, first, last):
                    if not first:
                        sp.wait_ge(rows_in[s], 16 * TILES * g)
                        stand(sp)
                        sp.wait_ge(attr_used, c - SLOTS + 1)
                        stand(sp)
                    sp.dma_start(src_idx[:, s, :], src_slots[bass.ds(c, 1), :, :].rearrange("o p j -> (o p) j")
                                 ).then_inc(src_in[s], 16)
                    if last:
                        at = [chunk_start(k, E) for k in range(NCH - SLOTS, NCH)][s]
                        edges = edge_attr[at:at + CHUNK, :]
                    else:
                        edges = edge_attr[bass.ds(c * CHUNK, CHUNK), :]
                    sp.dma_start(attr[:, s, :, :], edges.rearrange("(p j) k -> p j k", j=TILES)).then_inc(attr_in[s], 16)

                for s in range(SLOTS):
                    load(s, 0, s, True, False)
                with sp.Fori(1, GROUPS - 1) as g:
                    for s in range(SLOTS):
                        load(g * SLOTS + s, g, s, False, False)
                for s in range(SLOTS):
                    load(NCH - SLOTS + s, GROUPS - 1, s, False, True)

            @block.gpsimd
            def _(pool):
                def gather(c, g, s, first):
                    pool.wait_ge(src_in[s], 16 * (g + 1))
                    if not first:
                        pool.wait_ge(sums_ready, c - SLOTS + 1)
                    stand(pool)
                    for j in range(TILES):
                        pool.indirect_dma_start(rows[:, s, j, :], None, table,
                                                bass.IndirectOffsetOnAxis(ap=src_idx[:, s, j:j + 1], axis=0)
                                                ).then_inc(rows_in[s], 16)

                for s in range(SLOTS):
                    gather(s, 0, s, True)
                with pool.Fori(1, GROUPS) as g:
                    for s in range(SLOTS):
                        gather(g * SLOTS + s, g, s, False)

            @block.vector
            def _(dve):
                def chunk(c, g, s, last):
                    nxt = ((s + 1) % SLOTS, 16 * (g + (s + 1) // SLOTS + 1))
                    if has(c, 1):
                        dve.wait_ge(weights_ready, c)
                    compare(dve, c, dst_loc[:, bass.ds(c * TILES, TILES)])
                    add_scores(dve, s, c, 16 * TILES * (g + 1))
                    mask(dve, c, c)
                    if has(c, 1):
                        before = dve.value_load(base_i[0:1, bass.ds(c - 1, 1)], min_val=0, max_val=N - 1)
                        add_sums(dve, c - 1, (s - 1) % SLOTS, before)
                    chunk_maximum(dve, c)
                    if not last:
                        dot_attr(dve, *nxt, range(0, TILES // 2))
                    here = dve.value_load(base_i[0:1, bass.ds(c, 1)], min_val=0, max_val=N - 1)
                    grow_maximum(dve, c, s, here)
                    if not last:
                        dot_attr(dve, *nxt, range(TILES // 2, TILES))
                    dve.wait_ge(max_stored, c + 1)
                    stand(dve)

                dot_attr(dve, 0, 16, range(TILES))
                for s in range(SLOTS):
                    chunk(s, 0, s, False)
                nc.vector.tensor_scalar(in_flag[:], dst_loc[:], WINDOW - 0.5, None, ALU.is_lt).then_inc(counted, 1)
                dve.wait_ge(counted, 1)
                nc.vector.scalar_tensor_tensor(in_flag[:], dst_loc[:], -0.5, in_flag[:], ALU.is_gt, ALU.mult
                                               ).then_inc(counted, 1)
                dve.wait_ge(counted, 2)
                nc.vector.tensor_reduce(in_count[:], in_flag[:], AX.X, ALU.add).then_inc(counted, 1)
                with dve.Fori(1, GROUPS - 1) as g:
                    for s in range(SLOTS):
                        chunk(g * SLOTS + s, g, s, False)
                for s in range(SLOTS):
                    chunk(NCH - SLOTS + s, GROUPS - 1, s, s == SLOTS - 1)
                dve.wait_ge(count_spread, 1)
                nc.vector.tensor_scalar(outside_i[:], t_setup[1][:, 0:1], -1.0, float(E), ALU.mult, ALU.add
                                        ).then_inc(outside_ready, 1)
                end = dve.value_load(base_i[0:1, NCH - 1:NCH], min_val=0, max_val=N - 1)
                add_sums(dve, NCH - 1, (NCH - 1) % SLOTS, end)
                dve.wait_ge(sums_added, NCH)
                dve.wait_ge(outside_ready, 1)

            @block.tensor
            def _(pe):
                for s in range(SLOTS):
                    products(pe, s, s)
                pe.wait_ge(counted, 3)
                pe.matmul(t_setup[1][:, 0:1], ones[:], in_count[:], start=True, stop=True).then_inc(count_spread, 1)
                with pe.Fori(1, GROUPS) as g:
                    for s in range(SLOTS):
                        products(pe, g * SLOTS + s, s)

            @block.scalar
            def _(act):
                for s in range(SLOTS):
                    exponentials(act, s, s)
                with act.Fori(1, GROUPS) as g:
                    for s in range(SLOTS):
                        exponentials(act, g * SLOTS + s, s)

        with ExitStack() as st:
            block = st.enter_context(nc.Block())

            def if_outside(eng):
                outside = eng.value_load(outside_i[0:1, 0:1], min_val=0, max_val=E)
                return eng.If(outside > 0)

            @block.sync
            def _(sp):
                def load(c, edges):
                    sp.wait_ge(rows_in[0], 16 * TILES * (GROUPS + c))
                    stand(sp)
                    sp.wait_ge(attr_used, NCH + c)
                    stand(sp)
                    sp.dma_start(src_idx[:, 0, :], src_slots[bass.ds(c, 1), :, :].rearrange("o p j -> (o p) j")
                                 ).then_inc(src_in[0], 16)
                    sp.dma_start(attr[:, 0, :, :], edges.rearrange("(p j) k -> p j k", j=TILES)).then_inc(attr_in[0], 16)

                with if_outside(sp):
                    with sp.Fori(0, NCH - SLOTS) as c:
                        load(c, edge_attr[bass.ds(c * CHUNK, CHUNK), :])
                    for c in range(NCH - SLOTS, NCH):
                        at = chunk_start(c, E)
                        load(c, edge_attr[at:at + CHUNK, :])

            @block.gpsimd
            def _(pool):
                with if_outside(pool):
                    with pool.Fori(0, NCH) as c:
                        pool.wait_ge(src_in[0], 16 * (GROUPS + c + 1))
                        pool.wait_ge(sums_ready, NCH + c * WINDOWS)
                        stand(pool)
                        for j in range(TILES):
                            pool.indirect_dma_start(rows[:, 0, j, :], None, table,
                                                    bass.IndirectOffsetOnAxis(ap=src_idx[:, 0, j:j + 1], axis=0)
                                                    ).then_inc(rows_in[0], 16)

            @block.vector
            def _(dve):
                with if_outside(dve):
                    with dve.Fori(0, NCH) as c:
                        dot_attr(dve, 0, 16 * (GROUPS + c + 1), range(TILES))
                        add_scores(dve, 0, NCH + c, 16 * TILES * (GROUPS + c + 1))
                        dst_here = dst_loc[:, bass.ds(c * TILES, TILES)]
                        nc.vector.tensor_scalar(below_end[:], dst_here, WINDOW - 0.5, None, ALU.is_lt).then_inc(left_step, 1)
                        nc.vector.tensor_tensor(dst_left[:], dst_here,
                                                base_bc[:, bass.ds(c, 1)].to_broadcast([P, TILES]), ALU.add)
                        dve.wait_ge(left_step, 3 * c + 1)
                        nc.vector.scalar_tensor_tensor(in_window[:], dst_here, -0.5, below_end[:], ALU.is_gt, ALU.mult
                                                       ).then_inc(left_step, 1)
                        dve.wait_ge(left_step, 3 * c + 2)
                        nc.vector.scalar_tensor_tensor(dst_left[:], in_window[:], -float(1 << 20), dst_left[:],
                                                       ALU.mult, ALU.add).then_inc(left_step, 1)
                        dve.wait_ge(left_step, 3 * c + 3)
                        stand(dve)
                        with dve.Fori(0, WINDOWS) as w:
                            n = NCH + c * WINDOWS + w
                            compare(dve, n, dst_left[:])
                            dve.wait_ge(differs, n + 1)
                            nc.vector.tensor_scalar(dst_left[:], dst_left[:], float(WINDOW), None, ALU.subtract
                                                    ).then_inc(left_moved, 1)
                            mask(dve, n, NCH + c)
                            chunk_maximum(dve, n)
                            grow_maximum(dve, n, 0, w * WINDOW)
                            add_sums(dve, n, 0, w * WINDOW)
                            dve.wait_ge(sums_added, n + 1)
                            dve.wait_ge(left_moved, c * WINDOWS + w + 1)
                            stand(dve)

            @block.tensor
            def _(pe):
                with if_outside(pe):
                    with pe.Fori(0, NCH) as c:
                        with pe.Fori(0, WINDOWS) as w:
                            products(pe, NCH + c * WINDOWS + w, 0)

            @block.scalar
            def _(act):
                with if_outside(act):
                    with act.Fori(0, NCH) as c:
                        with act.Fori(0, WINDOWS) as w:
                            exponentials(act, NCH + c * WINDOWS + w, 0)

        chunk_stack.close()

        with ExitStack() as st:
            sums_here = slots(st, "sums_here", [P, H + 1, P])
            x_here = slots(st, "x_here", [P, D])
            gained = slots(st, "gained", [P, D])
            total = slots(st, "total", [P, 1])
            inverse = slots(st, "inverse", [P, 1])
            x_here_in = [sem(f"x_here_in{s}") for s in range(SLOTS)]
            out_stored = [sem(f"out_stored{s}") for s in range(SLOTS)]
            sums_taken = sem("sums_taken")
            projected = sem("projected")
            total_ready = sem("total_ready")
            inverse_ready = sem("inverse_ready")
            averaged = sem("averaged")
            added = sem("added")

            TURNS = (BLOCKS - 1) // SLOTS
            TAIL = range(TURNS * SLOTS, BLOCKS)

            def blocks_of(eng, body):
                for s in range(SLOTS):
                    body(s, 0, s, P)
                with eng.Fori(1, TURNS) as g:
                    for s in range(SLOTS):
                        body(g * SLOTS + s, g, s, P)
                for b in TAIL:
                    body(b, TURNS + (b - TAIL[0]) // SLOTS, b % SLOTS, min(P, N - b * P))

            def rows_at(ap, b, n):
                return ap[b * P:b * P + n, :] if isinstance(b, int) else ap[bass.ds(b * P, n), :]

            block = st.enter_context(nc.Block())

            @block.sync
            def _(sp):
                def load(b, g, s, n):
                    if has(b, SLOTS):
                        sp.wait_ge(added, b - SLOTS + 1)
                        stand(sp)
                    sp.dma_start(x_here[s][0:n, :], rows_at(x, b, n)).then_inc(x_here_in[s], 16)
                blocks_of(sp, load)

            @block.vector
            def _(dve):
                def take(b, g, s, n):
                    if has(b, SLOTS):
                        dve.wait_ge(projected, b - SLOTS + 1)
                        stand(dve)
                    nc.vector.tensor_copy(sums_here[s][:], sums[:, :, bass.ds(b * P, P)]).then_inc(sums_taken, 1)
                    dve.wait_ge(projected, b + 1)
                    if has(b, SLOTS):
                        dve.wait_ge(averaged, b - SLOTS + 1)
                    nc.vector.tensor_scalar(total[s][:], t_out[s][:, D:D + 1], DENOM_EPS, None, ALU.add).then_inc(total_ready, 1)
                    dve.wait_ge(total_ready, b + 1)
                    nc.vector.reciprocal(inverse[s][:], total[s][:]).then_inc(inverse_ready, 1)
                blocks_of(dve, take)

            @block.tensor
            def _(pe):
                def project(b, g, s, n):
                    pe.wait_ge(sums_taken, b + 1)
                    if has(b, SLOTS):
                        pe.wait_ge(averaged, b - SLOTS + 1)
                    for h in range(H):
                        pe.matmul(t_out[s][:, 0:D], sums_here[s][:, h, :], wnT_sb[:, h, :], start=(h == 0), stop=False)
                    pe.matmul(t_out[s][:, 0:D], sums_here[s][:, H, :], bn_rows[:], start=False, stop=True)
                    pe.matmul(t_out[s][:, D:D + 1], sums_here[s][:, H, :], first_row[:], start=True, stop=True
                              ).then_inc(projected, 1)
                blocks_of(pe, project)

            @block.scalar
            def _(act):
                def average(b, g, s, n):
                    act.wait_ge(inverse_ready, b + 1)
                    if has(b, SLOTS):
                        act.wait_ge(out_stored[s], 16 * g)
                    nc.scalar.activation(gained[s][:], t_out[s][:, 0:D], ACT.Relu, scale=inverse[s][:, 0:1]
                                         ).then_inc(averaged, 1)
                blocks_of(act, average)

            @block.gpsimd
            def _(pool):
                def add(b, g, s, n):
                    pool.wait_ge(averaged, b + 1)
                    pool.wait_ge(x_here_in[s], 16 * (g + 1))
                    nc.gpsimd.tensor_tensor(gained[s][0:n, :], gained[s][0:n, :], x_here[s][0:n, :], ALU.add
                                            ).then_inc(added, 1)
                    pool.wait_ge(added, b + 1)
                    stand(pool)
                    pool.dma_start(rows_at(out, b, n), gained[s][0:n, :]).then_inc(out_stored[s], 16)
                blocks_of(pool, add)
                for s in range(SLOTS):
                    pool.wait_ge(out_stored[s], 16 * len(range(s, BLOCKS, SLOTS)))
    return nc


def layout(src, dst):
    import numpy as np
    E = src.shape[0]
    n = chunks_of(E)
    start = np.array([chunk_start(c, E) for c in range(n)])
    edge = start[:, None, None] + np.arange(P)[:, None] * TILES + np.arange(TILES)
    repeated = edge < (np.arange(n) * CHUNK)[:, None, None]
    src_slots = np.ascontiguousarray(src[edge])
    dst_slots = np.where(repeated, np.int32(-1), dst[edge])
    return src_slots, np.ascontiguousarray(dst_slots.transpose(1, 0, 2).reshape(P, n * TILES))


def kernel(x, src, dst, edge_attr_128, L0_gnn_Wn, L0_gnn_bn, L0_gnn_We, L0_gnn_be, L0_gnn_attn):
    import numpy as np
    from concourse import bacc
    from concourse.bass_utils import run_bass_kernel_spmd

    src_slots, dst_slots = layout(np.asarray(src), np.asarray(dst))
    vectors = np.stack([np.asarray(v).reshape(-1, P).T for v in (L0_gnn_attn, L0_gnn_bn, L0_gnn_be)], axis=1)
    arrays = {
        "x": x, "src_slots": src_slots, "dst_slots": dst_slots, "edge_attr": edge_attr_128,
        "Wn": L0_gnn_Wn, "WnT": np.ascontiguousarray(np.asarray(L0_gnn_Wn).T), "We": L0_gnn_We,
        "bn": L0_gnn_bn, "vectors": vectors,
    }
    arrays = {k: np.ascontiguousarray(a) for k, a in arrays.items()}
    nc = bacc.Bacc("TRN2", target_bir_lowering=False, num_devices=1)
    aps = [nc.dram_tensor(f"in_{k}", a.shape, mybir.dt.from_np(a.dtype), kind="ExternalInput").ap()
           for k, a in arrays.items()]
    out = nc.dram_tensor("out", arrays["x"].shape, F32, kind="ExternalOutput").ap()
    gnn_layer(nc, *aps, out)
    r = run_bass_kernel_spmd(nc, [{f"in_{k}": a for k, a in arrays.items()}], core_ids=[0])
    return r.results[0]["out"]
```

```python
from contextlib import ExitStack

import concourse.bass as bass
from concourse import mybir

ALU = mybir.AluOpType
ACT = mybir.ActivationFunctionType
AX = mybir.AxisListType
F32 = mybir.dt.float32
I32 = mybir.dt.int32

P = 128
TILES = 12
SLOTS = 3
WINDOW = 64
CHUNK = TILES * P
NODES_PER_ROW = 7
ROW_PAD = 8
NEG_SLOPE = 0.01
LN_EPS = 1e-5
DENOM_EPS = 1e-16
MASKED = -(2.0 ** 100)
NO_MAX = -(2.0 ** 90)


def chunks_of(n_edges):
    n = -(-n_edges // CHUNK)
    return -(-n // SLOTS) * SLOTS


def chunk_start(c, n_edges):
    return min(c * CHUNK, n_edges - CHUNK)


class FinishSemaphores:

    def __init__(self, sem, run):
        self.x_in = [sem(f"{run}_x_in{s}") for s in range(SLOTS)]
        self.stored = [sem(f"{run}_stored{s}") for s in range(SLOTS)]
        self.taken = sem(f"{run}_taken")
        self.projected = sem(f"{run}_projected")
        self.totalled = sem(f"{run}_totalled")
        self.inverted = sem(f"{run}_inverted")
        self.averaged = sem(f"{run}_averaged")
        self.added = sem(f"{run}_added")


def gnn_layer(nc, x, src_slots, dst_slots, edge_attr, Wn, WnT, We, bn, vectors, out):
    N, D = x.shape
    E, DE = edge_attr.shape
    ROW = D + ROW_PAD
    ONE, SCORE = D, D + 1
    NCH = chunks_of(E)
    FULL = E // CHUNK
    GROUPS = NCH // SLOTS
    H = D // P
    GROUP_NODES = NODES_PER_ROW * P
    TABLE_GROUPS = -(-N // GROUP_NODES)
    BLOCKS = -(-N // P)
    WINDOWS = -(-N // WINDOW)
    NODE_COLS = BLOCKS * P + WINDOW
    SEL_EDGES = NCH * TILES
    assert D == 2 * P and DE == P and N >= GROUP_NODES and E >= CHUNK and NCH <= 512

    table = nc.dram_tensor("row_table", [N, ROW], F32, kind="Internal").ap()

    with ExitStack() as ctx:
        def sb(name, shape, dt=F32):
            return ctx.enter_context(nc.sbuf_tensor(name, shape, dt))

        def slots(stack, name, shape):
            return [stack.enter_context(nc.sbuf_tensor(f"{name}{s}", shape, F32)) for s in range(SLOTS)]

        def ps(name, shape):
            return ctx.enter_context(nc.psum_tensor(name, shape, F32))

        def sem(name):
            return ctx.enter_context(nc.semaphore(name))

        ident = sb("ident", [P, P])
        ones = sb("ones", [P, P])
        last_row = sb("last_row", [P, P])
        node_iota = sb("node_iota", [P, WINDOW])
        wn_sb = sb("wn_sb", [P, H, D])
        finish_w = sb("finish_w", [P, H + 1, D + 1])
        we_sb = sb("we_sb", [P, H, DE])
        cols = sb("cols", [P, 3, H])
        attn_wide = sb("attn_wide", [P, H, P])
        u_bc = sb("u_bc", [P, D])
        v_bc = sb("v_bc", [P, DE])
        score_const = sb("score_const", [P, 2])
        dst_loc = sb("dst_loc", [P, SEL_EDGES])
        base_bc = sb("base_bc", [P, NCH])
        base_i = sb("base_i", [P, NCH], I32)
        src_idx = sb("src_idx", [P, SLOTS, TILES], I32)
        node_max = sb("node_max", [P, NODE_COLS])
        sums = sb("sums", [P, H + 1, NODE_COLS])
        tile_max = sb("tile_max", [P, P])
        node_sums = sb("node_sums", [P, (H + 1) * P])
        finished_below = sb("finished_below", [P, NCH])
        outside_i = sb("outside_i", [P, 1], I32)
        sums_here = slots(ctx, "sums_here", [P, H + 1, P])
        x_here = slots(ctx, "x_here", [P, D])
        gained = slots(ctx, "gained", [P, D])
        total = slots(ctx, "total", [P, 1])
        inverse = slots(ctx, "inverse", [P, 1])
        dst_left = sb("dst_left", [P, TILES])
        below_end = sb("below_end", [P, TILES])
        in_window = sb("in_window", [P, TILES])

        t_maxT = ps("t_maxT", [P, P])
        t_maxB = ps("t_maxB", [P, WINDOW])
        t_node = ps("t_node", [P, D + 1])
        t_sums = ps("t_sums", [P, H + 1, P])
        t_out = [ps(f"t_out{s}", [P, 512]) for s in range(SLOTS)]

        t_setup = [t_out[0], t_out[1]]

        weights_in = sem("weights_in")
        dst_in = sem("dst_in")
        consts_ready = sem("consts_ready")
        ident_ready = sem("ident_ready")
        state_ready = sem("state_ready")
        src_in = [sem(f"src_in{s}") for s in range(SLOTS)]
        attr_in = [sem(f"attr_in{s}") for s in range(SLOTS)]
        rows_in = [sem(f"rows_in{s}") for s in range(SLOTS)]
        once = FinishSemaphores(sem, "once")
        again = FinishSemaphores(sem, "again")
        setup_step = sem("setup_step")
        attn_ready = sem("attn_ready")
        spread_ready = sem("spread_ready")
        vectors_ready = sem("vectors_ready")
        dst_float = sem("dst_float")
        base_spread = sem("base_spread")
        x_in = [sem(f"x_in{s}") for s in range(2)]
        stats_ready = sem("stats_ready")
        norm_step = sem("norm_step")
        var_ready = sem("var_ready")
        dev_ready = sem("dev_ready")
        norm_ready = sem("norm_ready")
        normed = sem("normed")
        row_ready = sem("row_ready")
        table_out = [sem(f"table_out{s}") for s in range(2)]
        attr_used = sem("attr_used")
        summed = sem("summed")
        scored = sem("scored")
        differs = sem("differs")
        masked_ready = sem("masked_ready")
        tile_max_ready = sem("tile_max_ready")
        maxT_ready = sem("maxT_ready")
        chunk_max_ready = sem("chunk_max_ready")
        diag_ready = sem("diag_ready")
        maxB_ready = sem("maxB_ready")
        new_max_ready = sem("new_max_ready")
        drop_ready = sem("drop_ready")
        max_stored = sem("max_stored")
        shifted = sem("shifted")
        decay_ready = sem("decay_ready")
        weights_ready = sem("weights_ready")
        multiplied = sem("multiplied")
        node_sums_ready = sem("node_sums_ready")
        sums_ready = sem("sums_ready")
        decayed = sem("decayed")
        sums_added = sem("sums_added")
        counted = sem("counted")
        count_spread = sem("count_spread")
        outside_ready = sem("outside_ready")
        left_step = sem("left_step")
        left_moved = sem("left_moved")
        passed = sem("passed")

        def stand(eng):
            eng.sem_inc(passed, 1)

        def per_tile(ap):
            return ap.unsqueeze(2).to_broadcast([P, TILES, WINDOW])

        def per_node(ap):
            return ap.unsqueeze(1).to_broadcast([P, TILES, WINDOW])

        def has(c, n):
            return not isinstance(c, int) or c >= n

        with ExitStack() as st:
            x_rows = [st.enter_context(nc.sbuf_tensor(f"x_rows{s}", [P, NODES_PER_ROW, D], F32)) for s in range(2)]
            t_rows = [st.enter_context(nc.sbuf_tensor(f"t_rows{s}", [P, NODES_PER_ROW, ROW], F32)) for s in range(2)]
            stats = [st.enter_context(nc.sbuf_tensor(f"stats{s}", [P, NODES_PER_ROW, 6], F32)) for s in range(2)]
            mean_var = [st.enter_context(nc.sbuf_tensor(f"mean_var{s}", [P, NODES_PER_ROW, 2], F32)) for s in range(2)]
            var_eps = [st.enter_context(nc.sbuf_tensor(f"var_eps{s}", [P, NODES_PER_ROW], F32)) for s in range(2)]
            dev = [st.enter_context(nc.sbuf_tensor(f"dev{s}", [P, NODES_PER_ROW], F32)) for s in range(2)]
            rstd = [st.enter_context(nc.sbuf_tensor(f"rstd{s}", [P, NODES_PER_ROW], F32)) for s in range(2)]
            shift = [st.enter_context(nc.sbuf_tensor(f"shift{s}", [P, NODES_PER_ROW], F32)) for s in range(2)]
            dst_i = st.enter_context(nc.sbuf_tensor("dst_i", [P, SEL_EDGES], I32))
            scrap = st.enter_context(nc.sbuf_tensor("scrap", [P, NODES_PER_ROW, D], F32))

            def node_group(ap, q):
                at = min(q * GROUP_NODES, N - GROUP_NODES)
                return ap[at:at + GROUP_NODES, :].rearrange("(p r) c -> p r c", r=NODES_PER_ROW)

            block = st.enter_context(nc.Block())

            @block.sync
            def _(sp):
                for q in range(TABLE_GROUPS):
                    if q >= 2:
                        sp.wait_ge(row_ready, q - 1)
                    sp.dma_start(x_rows[q % 2][:], node_group(x, q)).then_inc(x_in[q % 2], 16)
                    if q == 0:
                        sp.dma_start(cols[:], vectors).then_inc(weights_in, 16)
                        sp.dma_start(wn_sb[:], Wn.rearrange("(h p) i -> p h i", p=P)).then_inc(weights_in, 16)
                        sp.dma_start(we_sb[:], We.rearrange("(h p) i -> p h i", p=P)).then_inc(weights_in, 16)
                        sp.dma_start(dst_i[:], dst_slots).then_inc(dst_in, 16)
                        sp.wait_ge(state_ready, 1)
                        sp.dma_start(finish_w[:, 0:H, 0:D], WnT.rearrange("(h p) o -> p h o", p=P)).then_inc(dst_in, 16)
                        sp.dma_start(finish_w[0:1, H, 0:D], bn.rearrange("(a d) -> a d", a=1)).then_inc(dst_in, 16)

            @block.gpsimd
            def _(pool):
                nc.gpsimd.memset(ones[:], 1.0)
                nc.gpsimd.memset(ident[:], 0.0)
                nc.gpsimd.memset(last_row[:], 0.0)
                nc.gpsimd.memset(node_sums[:], 0.0)
                nc.gpsimd.memset(tile_max[:], 0.0)
                for s in range(2):
                    nc.gpsimd.memset(t_rows[s][:, :, D:ROW], 0.0)
                nc.gpsimd.iota(finished_below[:], pattern=[[P, GROUPS], [0, SLOTS]], base=0, channel_multiplier=0,
                               allow_small_or_imprecise_dtypes=True)
                nc.gpsimd.iota(node_iota[:], pattern=[[1, WINDOW]], base=0, channel_multiplier=0,
                               allow_small_or_imprecise_dtypes=True)
                nc.gpsimd.memset(finish_w[:], 0.0).then_inc(state_ready, 1)
                pool.wait_ge(state_ready, 1)
                nc.gpsimd.affine_select(out=ident[:], in_=ident[:], compare_op=ALU.not_equal, fill=1.0,
                                        base=0, pattern=[[-1, P]], channel_multiplier=1)
                nc.gpsimd.affine_select(out=last_row[:], in_=last_row[:], compare_op=ALU.not_equal, fill=1.0,
                                        base=-(P - 1), pattern=[[0, P]], channel_multiplier=1)
                nc.gpsimd.affine_select(out=finish_w[:, H, D:D + 1], in_=finish_w[:, H, D:D + 1],
                                        compare_op=ALU.not_equal, fill=1.0,
                                        base=0, pattern=[[0, 1]], channel_multiplier=1)
                for s in range(2):
                    last = nc.gpsimd.memset(t_rows[s][:, :, ONE:ONE + 1], 1.0)
                last.then_inc(consts_ready, 1)
                nc.gpsimd.memset(node_max[:], NO_MAX)
                nc.gpsimd.memset(sums[:], 0.0).then_inc(state_ready, 1)

            @block.tensor
            def _(pe):
                pe.wait_ge(consts_ready, 1)
                pe.wait_ge(weights_in, 3 * 16)
                pe.wait_ge(attn_ready, 1)
                for h in range(H):
                    pe.matmul(t_setup[0][:, 0:D], attn_wide[:, h, :], wn_sb[:, h, :], start=(h == 0), stop=(h == H - 1))
                for h in range(H):
                    pe.matmul(t_setup[0][:, D:D + DE], attn_wide[:, h, :], we_sb[:, h, :], start=(h == 0), stop=(h == H - 1))
                for h in range(H):
                    mm = pe.matmul(t_setup[0][:, D + DE:D + DE + 2], attn_wide[:, h, :], cols[:, 1:3, h],
                                   start=(h == 0), stop=(h == H - 1))
                mm.then_inc(spread_ready, 1)
                pe.wait_ge(dst_float, 1)
                pe.matmul(t_setup[1][:, 0:NCH], last_row[:],
                          dst_loc[:].rearrange("p (c j) -> p c j", j=TILES)[:, :, TILES - 1],
                          start=True, stop=True).then_inc(base_spread, 1)

            def stats_of(dve, q):
                s = q % 2
                dve.wait_ge(x_in[s], 16 * (q // 2 + 1))
                for r in range(NODES_PER_ROW):
                    last = nc.vector.bn_stats(stats[s][:, r, :], x_rows[s][:, r, :])
                last.then_inc(stats_ready, 1)
                dve.wait_ge(stats_ready, q + 1)
                for r in range(NODES_PER_ROW):
                    last = nc.vector.bn_aggr(mean_var[s][:, r, :], stats[s][:, r, :])
                last.then_inc(norm_step, 1)
                dve.wait_ge(norm_step, 2 * q + 1)
                if q >= 2:
                    dve.wait_ge(normed, q - 1)
                nc.vector.tensor_scalar(var_eps[s][:], mean_var[s][:, :, 1], LN_EPS, None, ALU.add).then_inc(var_ready, 1)

            def shift_of(dve, q):
                s = q % 2
                dve.wait_ge(dev_ready, q + 1)
                nc.vector.reciprocal(rstd[s][:], dev[s][:]).then_inc(norm_step, 1)
                dve.wait_ge(norm_step, 2 * q + 2)
                nc.vector.scalar_tensor_tensor(shift[s][:], mean_var[s][:, :, 0], -1.0, rstd[s][:],
                                               ALU.mult, ALU.mult).then_inc(norm_ready, 1)

            def node_scores(dve, q):
                s = q % 2
                dve.wait_ge(normed, q + 1)
                if q >= 1:
                    dve.wait_ge(row_ready, q)
                for r in range(NODES_PER_ROW):
                    last = nc.vector.tensor_tensor_reduce(scrap[:, r, :], t_rows[s][:, r, 0:D], u_bc[:], 1.0,
                                                          score_const[:, 0:1], ALU.mult, ALU.add,
                                                          t_rows[s][:, r, SCORE:SCORE + 1])
                last.then_inc(row_ready, 1)

            @block.vector
            def _(dve):
                dve.wait_ge(consts_ready, 1)
                dve.wait_ge(weights_in, 3 * 16)
                for h in range(H):
                    last = nc.vector.tensor_scalar(attn_wide[:, h, :], ones[:], cols[:, 0, h:h + 1], None, ALU.mult)
                last.then_inc(attn_ready, 1)
                stats_of(dve, 0)
                shift_of(dve, 0)
                dve.wait_ge(spread_ready, 1)
                nc.vector.tensor_copy(u_bc[:], t_setup[0][:, 0:D])
                nc.vector.tensor_copy(v_bc[:], t_setup[0][:, D:D + DE])
                nc.vector.tensor_copy(score_const[:], t_setup[0][:, D + DE:D + DE + 2]).then_inc(setup_step, 1)
                dve.wait_ge(setup_step, 1)
                nc.vector.tensor_tensor(score_const[:, 0:1], score_const[:, 0:1], score_const[:, 1:2],
                                        ALU.add).then_inc(vectors_ready, 1)
                dve.wait_ge(vectors_ready, 1)
                for q in range(TABLE_GROUPS):
                    if q + 1 < TABLE_GROUPS:
                        stats_of(dve, q + 1)
                    node_scores(dve, q)
                    if q + 1 < TABLE_GROUPS:
                        shift_of(dve, q + 1)
                dve.wait_ge(dst_in, 3 * 16)
                nc.vector.tensor_copy(dst_loc[:], dst_i[:]).then_inc(dst_float, 1)
                dve.wait_ge(base_spread, 1)
                nc.vector.tensor_scalar(base_bc[:], t_setup[1][:, 0:NCH], float(WINDOW - 1), 0.0,
                                        ALU.subtract, ALU.max).then_inc(setup_step, 1)
                dve.wait_ge(setup_step, 2)
                nc.vector.tensor_copy(base_i[:], base_bc[:])
                dst_by_chunk = dst_loc[:].rearrange("p (c j) -> p c j", j=TILES)
                nc.vector.tensor_tensor(dst_by_chunk, dst_by_chunk,
                                        base_bc[:].unsqueeze(2).to_broadcast([P, NCH, TILES]),
                                        ALU.subtract).then_inc(setup_step, 1)
                dve.wait_ge(setup_step, 3)

            def store(act, q):
                act.wait_ge(row_ready, q + 1)
                if q == TABLE_GROUPS - 1:
                    act.wait_ge(table_out[(q - 1) % 2], 16 * ((q - 1) // 2 + 1))
                act.dma_start(node_group(table, q), t_rows[q % 2][:]).then_inc(table_out[q % 2], 16)

            @block.scalar
            def _(act):
                def deviation(q):
                    act.wait_ge(var_ready, q + 1)
                    nc.scalar.activation(dev[q % 2][:], var_eps[q % 2][:], ACT.Sqrt).then_inc(dev_ready, 1)

                deviation(0)
                for q in range(TABLE_GROUPS):
                    s = q % 2
                    act.wait_ge(norm_ready, q + 1)
                    if q == 0:
                        act.wait_ge(consts_ready, 1)
                    if q >= 2:
                        act.wait_ge(table_out[s], 16 * (q // 2))
                    for r in range(NODES_PER_ROW):
                        last = nc.scalar.activation(t_rows[s][:, r, 0:D], x_rows[s][:, r, :], ACT.Relu,
                                                    bias=shift[s][:, r:r + 1], scale=rstd[s][:, r:r + 1])
                    last.then_inc(normed, 1)
                    if q + 1 < TABLE_GROUPS:
                        deviation(q + 1)
                    if q >= 1:
                        store(act, q - 1)
                store(act, TABLE_GROUPS - 1)
                for s in range(2):
                    act.wait_ge(table_out[s], 16 * ((TABLE_GROUPS + 1 - s) // 2))

        chunk_stack = ctx.enter_context(ExitStack())

        def chunk_sb(name, shape, dt=F32):
            return chunk_stack.enter_context(nc.sbuf_tensor(name, shape, dt))

        rows = chunk_sb("rows", [P, SLOTS, TILES, ROW])
        attr = chunk_sb("attr", [P, SLOTS, TILES, DE])
        attr_dot = chunk_sb("attr_dot", [P, TILES])
        score_sum = chunk_sb("score_sum", [P, TILES])
        score = chunk_sb("score", [P, TILES])
        masked = chunk_sb("masked", [P, TILES, WINDOW])
        weights = chunk_sb("weights", [P, SLOTS, TILES, WINDOW])
        chunk_max = chunk_sb("chunk_max", [WINDOW, 1])
        max_diag = chunk_sb("max_diag", [WINDOW, WINDOW])
        new_max = chunk_sb("new_max", [P, WINDOW])
        max_drop = chunk_sb("max_drop", [P, SLOTS, WINDOW])
        decay = chunk_sb("decay", [P, SLOTS, WINDOW])
        in_flag = chunk_sb("in_flag", [P, SEL_EDGES])
        in_count = chunk_sb("in_count", [P, 1])

        def rows_at(ap, b, n):
            return ap[b * P:b * P + n, :] if isinstance(b, int) else ap[bass.ds(b * P, n), :]

        def load_x(eng, f, m, before, s, turn, b, n):
            if before is not None:
                eng.wait_ge(f.added, before)
                stand(eng)
            eng.dma_start(x_here[s][0:n, :], rows_at(x, b, n)).then_inc(f.x_in[s], 16)

        def take_sums(dve, f, m, before, s, turn, b, n):
            if before is not None:
                dve.wait_ge(f.projected, before)
                stand(dve)
            nc.vector.tensor_copy(sums_here[s][:], sums[:, :, bass.ds(b * P, P)]).then_inc(f.taken, 1)

        def project(pe, f, m, before, s, turn, b, n):
            pe.wait_ge(f.taken, m + 1)
            if before is not None:
                pe.wait_ge(f.averaged, before)
            for h in range(H + 1):
                mm = pe.matmul(t_out[s][:, 0:D + 1], sums_here[s][:, h, :], finish_w[:, h, :],
                               start=(h == 0), stop=(h == H))
            mm.then_inc(f.projected, 1)

        def invert(dve, f, m, before, s, turn, b, n):
            dve.wait_ge(f.projected, m + 1)
            if before is not None:
                dve.wait_ge(f.averaged, before)
            nc.vector.tensor_scalar(total[s][:], t_out[s][:, D:D + 1], DENOM_EPS, None, ALU.add).then_inc(f.totalled, 1)
            dve.wait_ge(f.totalled, m + 1)
            nc.vector.reciprocal(inverse[s][:], total[s][:]).then_inc(f.inverted, 1)

        def average(act, f, m, before, s, turn, b, n):
            act.wait_ge(f.inverted, m + 1)
            if before is not None:
                act.wait_ge(f.stored[s], 16 * turn)
            nc.scalar.activation(gained[s][:], t_out[s][:, 0:D], ACT.Relu, scale=inverse[s][:, 0:1]).then_inc(f.averaged, 1)

        def add_x(eng, f, m, before, s, turn, b, n):
            eng.wait_ge(f.averaged, m + 1)
            eng.wait_ge(f.x_in[s], 16 * (turn + 1))
            eng.tensor_tensor(gained[s][0:n, :], gained[s][0:n, :], x_here[s][0:n, :], ALU.add).then_inc(f.added, 1)

        def store(eng, f, m, before, s, turn, b, n):
            eng.wait_ge(f.added, m + 1)
            eng.dma_start(rows_at(out, b, n), gained[s][0:n, :]).then_inc(f.stored[s], 16)

        def in_turn(g):
            return g - 1, g - 1 if has(g, 2) else None, 0, g - 1, g - 1, P

        def dot_attr(dve, s, landed, tiles):
            if tiles[0] == 0:
                dve.wait_ge(attr_in[s], landed)
            for j in tiles:
                last = nc.vector.tensor_tensor_reduce(attr[:, s, j, :], attr[:, s, j, :], v_bc[:], 1.0, 0.0,
                                                      ALU.mult, ALU.add, attr_dot[:, j:j + 1])
            if tiles[-1] == TILES - 1:
                last.then_inc(attr_used, 1)

        def add_scores(dve, s, c, landed):
            dve.wait_ge(rows_in[s], landed)
            dve.wait_ge(attr_used, c + 1)
            nc.vector.tensor_tensor(score_sum[:], attr_dot[:], rows[:, s, :, SCORE], ALU.add).then_inc(summed, 1)
            dve.wait_ge(summed, c + 1)
            nc.vector.scalar_tensor_tensor(score[:], score_sum[:], NEG_SLOPE, score_sum[:],
                                           ALU.mult, ALU.max).then_inc(scored, 1)

        def compare(dve, c, dst_here):
            nc.vector.tensor_tensor(masked[:], per_node(node_iota[:]), per_tile(dst_here),
                                    ALU.not_equal).then_inc(differs, 1)

        def mask(dve, c, chunks):
            dve.wait_ge(differs, c + 1)
            dve.wait_ge(scored, chunks + 1)
            nc.vector.scalar_tensor_tensor(masked[:], masked[:], MASKED, per_tile(score[:]),
                                           ALU.mult, ALU.add).then_inc(masked_ready, 1)
            dve.wait_ge(masked_ready, c + 1)
            if has(c, 1):
                dve.wait_ge(maxT_ready, c)
            nc.vector.tensor_reduce(tile_max[:, 0:WINDOW], masked[:].rearrange("p j n -> p n j"),
                                    AX.X, ALU.max).then_inc(tile_max_ready, 1)

        def chunk_maximum(dve, c):
            dve.wait_ge(maxT_ready, c + 1)
            nc.vector.tensor_reduce(chunk_max[:], t_maxT[0:WINDOW, :], AX.X, ALU.max).then_inc(chunk_max_ready, 1)
            dve.wait_ge(chunk_max_ready, c + 1)
            if has(c, 1):
                dve.wait_ge(maxB_ready, c)
            nc.vector.tensor_scalar(max_diag[:], ident[0:WINDOW, 0:WINDOW], chunk_max[:, 0:1], None,
                                    ALU.mult).then_inc(diag_ready, 1)

        def grow_maximum(dve, c, s, first_node):
            here = node_max[:, bass.ds(first_node, WINDOW)]
            dve.wait_ge(maxB_ready, c + 1)
            nc.vector.tensor_tensor(new_max[:], here, t_maxB[:], ALU.max).then_inc(new_max_ready, 1)
            dve.wait_ge(new_max_ready, c + 1)
            if has(c, SLOTS):
                dve.wait_ge(decay_ready, c - SLOTS + 1)
            nc.vector.tensor_tensor(max_drop[:, s, :], here, new_max[:], ALU.subtract).then_inc(drop_ready, 1)
            nc.vector.tensor_tensor(masked[:], masked[:], per_node(new_max[:]), ALU.subtract).then_inc(shifted, 1)
            dve.wait_ge(drop_ready, c + 1)
            nc.vector.tensor_tensor(here, new_max[:], new_max[:], ALU.max).then_inc(max_stored, 1)

        def add_sums(dve, c, s, first_node):
            here = sums[:, :, bass.ds(first_node, WINDOW)]
            dve.wait_ge(decay_ready, c + 1)
            if has(c, 1):
                dve.wait_ge(sums_added, c)
            nc.vector.tensor_tensor(here, here, decay[:, s, :].unsqueeze(1).to_broadcast([P, H + 1, WINDOW]),
                                    ALU.mult).then_inc(decayed, 1)
            dve.wait_ge(decayed, c + 1)
            dve.wait_ge(sums_ready, c + 1)
            nc.vector.tensor_tensor(here, here, t_sums[:, :, 0:WINDOW], ALU.add).then_inc(sums_added, 1)

        def products(pe, c, s):
            pe.wait_ge(tile_max_ready, c + 1)
            if has(c, 1):
                pe.wait_ge(chunk_max_ready, c)
            pe.transpose(t_maxT[:], tile_max[:], ident[:]).then_inc(maxT_ready, 1)
            pe.wait_ge(diag_ready, c + 1)
            if has(c, 1):
                pe.wait_ge(new_max_ready, c)
            pe.matmul(t_maxB[:], ones[0:WINDOW, :], max_diag[:], start=True, stop=True).then_inc(maxB_ready, 1)
            pe.wait_ge(weights_ready, c + 1)
            for j in range(TILES):
                mm = pe.matmul(t_node[0:WINDOW, :], weights[:, s, j, :], rows[:, s, j, 0:D + 1],
                               start=(j == 0), stop=(j == TILES - 1))
            mm.then_inc(multiplied, 1)
            pe.wait_ge(node_sums_ready, c + 1)
            if has(c, 1):
                pe.wait_ge(sums_added, c)
            for h in range(H + 1):
                mm = pe.transpose(t_sums[:, h, :], node_sums[:, h * P:(h + 1) * P], ident[:])
            mm.then_inc(sums_ready, 1)

        def exponentials(act, c, s):
            act.wait_ge(drop_ready, c + 1)
            if has(c, SLOTS):
                act.wait_ge(decayed, c - SLOTS + 1)
                act.wait_ge(multiplied, c - SLOTS + 1)
            nc.scalar.activation(decay[:, s, :], max_drop[:, s, :], ACT.Exp).then_inc(decay_ready, 1)
            act.wait_ge(shifted, c + 1)
            nc.scalar.activation(weights[:, s, :, :], masked[:], ACT.Exp).then_inc(weights_ready, 1)
            act.wait_ge(multiplied, c + 1)
            if has(c, 1):
                act.wait_ge(sums_ready, c)
            nc.scalar.copy(node_sums[0:WINDOW, 0:D], t_node[0:WINDOW, 0:D])
            nc.scalar.copy(node_sums[0:WINDOW, D:D + P], t_node[0:WINDOW, D:D + 1].to_broadcast([WINDOW, P])
                           ).then_inc(node_sums_ready, 1)

        with ExitStack() as st:
            block = st.enter_context(nc.Block())

            @block.sync
            def _(sp):
                def load(c, g, s, first, last):
                    if not first:
                        sp.wait_ge(rows_in[s], 16 * TILES * g)
                        stand(sp)
                        sp.wait_ge(attr_used, c - SLOTS + 1)
                        stand(sp)
                    sp.dma_start(src_idx[:, s, :], src_slots[bass.ds(c, 1), :, :].rearrange("o p j -> (o p) j")
                                 ).then_inc(src_in[s], 16)
                    if last:
                        at = [chunk_start(k, E) for k in range(NCH - SLOTS, NCH)][s]
                        edges = edge_attr[at:at + CHUNK, :]
                    else:
                        edges = edge_attr[bass.ds(c * CHUNK, CHUNK), :]
                    sp.dma_start(attr[:, s, :, :], edges.rearrange("(p j) k -> p j k", j=TILES)).then_inc(attr_in[s], 16)

                for s in range(SLOTS):
                    load(s, 0, s, True, False)
                with sp.Fori(1, GROUPS - 1) as g:
                    for s in range(SLOTS):
                        load(g * SLOTS + s, g, s, False, False)
                for s in range(SLOTS):
                    load(NCH - SLOTS + s, GROUPS - 1, s, False, True)

            @block.gpsimd
            def _(pool):
                def gather(c, g, s, first):
                    pool.wait_ge(src_in[s], 16 * (g + 1))
                    if not first:
                        pool.wait_ge(multiplied, c - SLOTS + 1)
                    stand(pool)
                    for j in range(TILES):
                        pool.indirect_dma_start(rows[:, s, j, :], None, table,
                                                bass.IndirectOffsetOnAxis(ap=src_idx[:, s, j:j + 1], axis=0)
                                                ).then_inc(rows_in[s], 16)

                for s in range(SLOTS):
                    gather(s, 0, s, True)
                with pool.Fori(1, GROUPS) as g:
                    for s in range(SLOTS):
                        gather(g * SLOTS + s, g, s, False)

            @block.vector
            def _(dve):
                def chunk(c, g, s, last):
                    nxt = ((s + 1) % SLOTS, 16 * (g + (s + 1) // SLOTS + 1))
                    if has(c, 1):
                        dve.wait_ge(weights_ready, c)
                    compare(dve, c, dst_loc[:, bass.ds(c * TILES, TILES)])
                    add_scores(dve, s, c, 16 * TILES * (g + 1))
                    mask(dve, c, c)
                    if has(c, 1):
                        before = dve.value_load(base_i[0:1, bass.ds(c - 1, 1)], min_val=0, max_val=N - 1)
                        add_sums(dve, c - 1, (s - 1) % SLOTS, before)
                    if has(g, 1) and s == 0:
                        dve.wait_ge(sums_added, c)
                        take_sums(dve, once, *in_turn(g))
                    if has(g, 1) and s == 1:
                        invert(dve, once, *in_turn(g))
                    if has(g, 1) and s == 2:
                        add_x(dve, once, *in_turn(g))
                    chunk_maximum(dve, c)
                    if not last:
                        dot_attr(dve, *nxt, range(0, TILES // 2))
                    here = dve.value_load(base_i[0:1, bass.ds(c, 1)], min_val=0, max_val=N - 1)
                    grow_maximum(dve, c, s, here)
                    if not last:
                        dot_attr(dve, *nxt, range(TILES // 2, TILES))
                    dve.wait_ge(max_stored, c + 1)
                    stand(dve)

                dot_attr(dve, 0, 16, range(TILES))
                for s in range(SLOTS):
                    chunk(s, 0, s, False)
                nc.vector.tensor_tensor(finished_below[:], finished_below[:], base_bc[:], ALU.subtract).then_inc(counted, 1)
                dve.wait_ge(counted, 1)
                nc.vector.tensor_scalar(finished_below[:], finished_below[:], 0.0, None, ALU.max).then_inc(counted, 1)
                dve.wait_ge(counted, 2)
                nc.vector.tensor_tensor(in_flag[:].rearrange("p (c j) -> p c j", j=TILES),
                                        dst_loc[:].rearrange("p (c j) -> p c j", j=TILES),
                                        finished_below[:].unsqueeze(2).to_broadcast([P, NCH, TILES]),
                                        ALU.is_ge).then_inc(counted, 1)
                dve.wait_ge(counted, 3)
                nc.vector.scalar_tensor_tensor(in_flag[:], dst_loc[:], WINDOW - 0.5, in_flag[:], ALU.is_lt, ALU.mult
                                               ).then_inc(counted, 1)
                dve.wait_ge(counted, 4)
                nc.vector.tensor_reduce(in_count[:], in_flag[:], AX.X, ALU.add).then_inc(counted, 1)
                for s in range(SLOTS):
                    chunk(SLOTS + s, 1, s, False)
                with dve.Fori(2, GROUPS - 1) as g:
                    for s in range(SLOTS):
                        chunk(g * SLOTS + s, g, s, False)
                for s in range(SLOTS):
                    chunk(NCH - SLOTS + s, GROUPS - 1, s, s == SLOTS - 1)
                dve.wait_ge(count_spread, 1)
                nc.vector.tensor_scalar(outside_i[:], t_setup[1][:, 0:1], -1.0, float(E), ALU.mult, ALU.add
                                        ).then_inc(outside_ready, 1)
                end = dve.value_load(base_i[0:1, NCH - 1:NCH], min_val=0, max_val=N - 1)
                add_sums(dve, NCH - 1, (NCH - 1) % SLOTS, end)
                dve.wait_ge(sums_added, NCH)
                dve.wait_ge(outside_ready, 1)

            @block.tensor
            def _(pe):
                for s in range(SLOTS):
                    products(pe, s, s)

                def turn(g):
                    for s in range(SLOTS):
                        products(pe, g * SLOTS + s, s)
                        if s == 0:
                            project(pe, once, *in_turn(g))
                pe.wait_ge(counted, 5)
                pe.matmul(t_setup[1][:, 0:1], ones[:], in_count[:], start=True, stop=True).then_inc(count_spread, 1)
                turn(1)
                with pe.Fori(2, GROUPS) as g:
                    turn(g)

            @block.scalar
            def _(act):
                def turn(g):
                    for s in range(SLOTS):
                        exponentials(act, g * SLOTS + s, s)
                        if has(g, 2) and s == 0:
                            store(act, once, *in_turn(g - 1))
                        if has(g, 1) and s == 0:
                            load_x(act, once, *in_turn(g))
                        if has(g, 1) and s == 1:
                            average(act, once, *in_turn(g))

                turn(0)
                turn(1)
                with act.Fori(2, GROUPS) as g:
                    turn(g)

        with ExitStack() as st:
            block = st.enter_context(nc.Block())

            def if_outside(eng):
                outside = eng.value_load(outside_i[0:1, 0:1], min_val=0, max_val=E)
                return eng.If(outside > 0)

            @block.sync
            def _(sp):
                def load(c, edges):
                    sp.wait_ge(rows_in[0], 16 * TILES * (GROUPS + c))
                    stand(sp)
                    sp.wait_ge(attr_used, NCH + c)
                    stand(sp)
                    sp.dma_start(src_idx[:, 0, :], src_slots[bass.ds(c, 1), :, :].rearrange("o p j -> (o p) j")
                                 ).then_inc(src_in[0], 16)
                    sp.dma_start(attr[:, 0, :, :], edges.rearrange("(p j) k -> p j k", j=TILES)).then_inc(attr_in[0], 16)

                with if_outside(sp):
                    with sp.Fori(0, NCH - SLOTS) as c:
                        load(c, edge_attr[bass.ds(c * CHUNK, CHUNK), :])
                    for c in range(NCH - SLOTS, NCH):
                        at = chunk_start(c, E)
                        load(c, edge_attr[at:at + CHUNK, :])

            @block.gpsimd
            def _(pool):
                with if_outside(pool):
                    with pool.Fori(0, NCH) as c:
                        pool.wait_ge(src_in[0], 16 * (GROUPS + c + 1))
                        pool.wait_ge(multiplied, NCH + c * WINDOWS)
                        stand(pool)
                        for j in range(TILES):
                            pool.indirect_dma_start(rows[:, 0, j, :], None, table,
                                                    bass.IndirectOffsetOnAxis(ap=src_idx[:, 0, j:j + 1], axis=0)
                                                    ).then_inc(rows_in[0], 16)

            @block.vector
            def _(dve):
                with if_outside(dve):
                    with dve.Fori(0, NCH) as c:
                        dot_attr(dve, 0, 16 * (GROUPS + c + 1), range(TILES))
                        add_scores(dve, 0, NCH + c, 16 * TILES * (GROUPS + c + 1))
                        dst_here = dst_loc[:, bass.ds(c * TILES, TILES)]
                        nc.vector.tensor_scalar(below_end[:], dst_here, WINDOW - 0.5, None, ALU.is_lt).then_inc(left_step, 1)
                        nc.vector.tensor_tensor(dst_left[:], dst_here,
                                                base_bc[:, bass.ds(c, 1)].to_broadcast([P, TILES]), ALU.add)
                        dve.wait_ge(left_step, 3 * c + 1)
                        nc.vector.scalar_tensor_tensor(in_window[:], dst_here, -0.5, below_end[:], ALU.is_gt, ALU.mult
                                                       ).then_inc(left_step, 1)
                        dve.wait_ge(left_step, 3 * c + 2)
                        nc.vector.scalar_tensor_tensor(dst_left[:], in_window[:], -float(1 << 20), dst_left[:],
                                                       ALU.mult, ALU.add).then_inc(left_step, 1)
                        dve.wait_ge(left_step, 3 * c + 3)
                        stand(dve)
                        with dve.Fori(0, WINDOWS) as w:
                            n = NCH + c * WINDOWS + w
                            compare(dve, n, dst_left[:])
                            dve.wait_ge(differs, n + 1)
                            nc.vector.tensor_scalar(dst_left[:], dst_left[:], float(WINDOW), None, ALU.subtract
                                                    ).then_inc(left_moved, 1)
                            mask(dve, n, NCH + c)
                            chunk_maximum(dve, n)
                            grow_maximum(dve, n, 0, w * WINDOW)
                            add_sums(dve, n, 0, w * WINDOW)
                            dve.wait_ge(sums_added, n + 1)
                            dve.wait_ge(left_moved, c * WINDOWS + w + 1)
                            stand(dve)

            @block.tensor
            def _(pe):
                with if_outside(pe):
                    with pe.Fori(0, NCH) as c:
                        with pe.Fori(0, WINDOWS) as w:
                            products(pe, NCH + c * WINDOWS + w, 0)

            @block.scalar
            def _(act):
                with if_outside(act):
                    with act.Fori(0, NCH) as c:
                        with act.Fori(0, WINDOWS) as w:
                            exponentials(act, NCH + c * WINDOWS + w, 0)

        chunk_stack.close()

        with ExitStack() as st:
            block = st.enter_context(nc.Block())
            DONE = GROUPS - 1
            AGAIN = DONE // SLOTS * SLOTS

            def finish_again(eng, *steps):
                def do(m, before, s, turn):
                    for step in steps:
                        step(eng, again, m, before, s, turn, m, P)
                with if_outside(eng):
                    for s in range(SLOTS):
                        do(s, None, s, 0)
                    with eng.Fori(1, AGAIN // SLOTS) as g:
                        for s in range(SLOTS):
                            do(g * SLOTS + s, g * SLOTS + s - SLOTS + 1, s, g)
                    for m in range(AGAIN, DONE):
                        do(m, m - SLOTS + 1, m % SLOTS, m // SLOTS)
                    eng.wait_ge(again.projected, DONE)
                    eng.wait_ge(again.averaged, DONE)
                    for s in range(SLOTS):
                        eng.wait_ge(again.stored[s], 16 * len(range(s, DONE, SLOTS)))
                    stand(eng)

            def finish_rest(eng, *steps):
                for i, b in enumerate(range(DONE, BLOCKS)):
                    s = i % SLOTS
                    before = DONE + i - SLOTS + 1 if i >= SLOTS else DONE if s == 0 else None
                    turn = i // SLOTS + (DONE if s == 0 else 0)
                    for step in steps:
                        step(eng, once, DONE + i, before, s, turn, b, min(P, N - b * P))

            @block.sync
            def _(sp):
                store(sp, once, *in_turn(DONE))
                sp.wait_ge(once.stored[0], 16 * DONE)
                finish_again(sp, store)
                finish_rest(sp, store)
                for s in range(SLOTS):
                    sp.wait_ge(once.stored[s], 16 * (len(range(s, BLOCKS - DONE, SLOTS)) + (DONE if s == 0 else 0)))

            @block.tensor
            def _(pe):
                finish_again(pe, project)
                finish_rest(pe, project)

            @block.vector
            def _(dve):
                finish_again(dve, take_sums, invert)
                finish_rest(dve, take_sums, invert)

            @block.scalar
            def _(act):
                act.wait_ge(once.stored[0], 16 * DONE)
                finish_again(act, load_x, average)
                finish_rest(act, load_x, average)

            @block.gpsimd
            def _(pool):
                finish_again(pool, add_x)
                finish_rest(pool, add_x)
    return nc


def layout(src, dst):
    import numpy as np
    E = src.shape[0]
    n = chunks_of(E)
    start = np.array([chunk_start(c, E) for c in range(n)])
    edge = start[:, None, None] + np.arange(P)[:, None] * TILES + np.arange(TILES)
    repeated = edge < (np.arange(n) * CHUNK)[:, None, None]
    src_slots = np.ascontiguousarray(src[edge])
    dst_slots = np.where(repeated, np.int32(-1), dst[edge])
    return src_slots, np.ascontiguousarray(dst_slots.transpose(1, 0, 2).reshape(P, n * TILES))


def kernel(x, src, dst, edge_attr_128, L0_gnn_Wn, L0_gnn_bn, L0_gnn_We, L0_gnn_be, L0_gnn_attn):
    import numpy as np
    from concourse import bacc
    from concourse.bass_utils import run_bass_kernel_spmd

    src_slots, dst_slots = layout(np.asarray(src), np.asarray(dst))
    vectors = np.stack([np.asarray(v).reshape(-1, P).T for v in (L0_gnn_attn, L0_gnn_bn, L0_gnn_be)], axis=1)
    arrays = {
        "x": x, "src_slots": src_slots, "dst_slots": dst_slots, "edge_attr": edge_attr_128,
        "Wn": L0_gnn_Wn, "WnT": np.ascontiguousarray(np.asarray(L0_gnn_Wn).T), "We": L0_gnn_We,
        "bn": L0_gnn_bn, "vectors": vectors,
    }
    arrays = {k: np.ascontiguousarray(a) for k, a in arrays.items()}
    nc = bacc.Bacc("TRN2", target_bir_lowering=False, num_devices=1)
    aps = [nc.dram_tensor(f"in_{k}", a.shape, mybir.dt.from_np(a.dtype), kind="ExternalInput").ap()
           for k, a in arrays.items()]
    out = nc.dram_tensor("out", arrays["x"].shape, F32, kind="ExternalOutput").ap()
    gnn_layer(nc, *aps, out)
    r = run_bass_kernel_spmd(nc, [{f"in_{k}": a for k, a in arrays.items()}], core_ids=[0])
    return r.results[0]["out"]
```

```python
from contextlib import ExitStack

import concourse.bass as bass
from concourse import mybir

ALU = mybir.AluOpType
ACT = mybir.ActivationFunctionType
AX = mybir.AxisListType
F32 = mybir.dt.float32
I32 = mybir.dt.int32

P = 128
TILES = 12
SLOTS = 3
WINDOW = 64
CHUNK = TILES * P
GROUP_ROWS = 8
ROW_PAD = 8
NEG_SLOPE = 0.01
LN_EPS = 1e-5
DENOM_EPS = 1e-16
MASKED = -(2.0 ** 100)
NO_MAX = -(2.0 ** 90)


def chunks_of(n_edges):
    n = -(-n_edges // CHUNK)
    return -(-n // SLOTS) * SLOTS


def first_tile(c, n_edges):
    return TILES - min(TILES, max(1, -(-(n_edges - c * CHUNK) // P)))


def chunk_start(c, n_edges):
    return min(c * CHUNK, n_edges - (TILES - first_tile(c, n_edges)) * P)


def table_groups(rows_each):
    if rows_each <= GROUP_ROWS:
        return [(0, rows_each)]
    ends = (2, 3)
    middle = rows_each - sum(ends)
    n = -(-middle // GROUP_ROWS)
    counts = [ends[0]] + [middle // n + (i < middle % n) for i in range(n)] + [ends[1]]
    return [(sum(counts[:i]), count) for i, count in enumerate(counts)]


class FinishSemaphores:

    def __init__(self, sem, run):
        self.x_in = [sem(f"{run}_x_in{s}") for s in range(SLOTS)]
        self.stored = [sem(f"{run}_stored{s}") for s in range(SLOTS)]
        self.taken = sem(f"{run}_taken")
        self.projected = sem(f"{run}_projected")
        self.totalled = sem(f"{run}_totalled")
        self.inverted = sem(f"{run}_inverted")
        self.averaged = sem(f"{run}_averaged")
        self.added = sem(f"{run}_added")


def gnn_layer(nc, x, src_slots, dst_slots, edge_attr, Wn, WnT, We, bn, vectors, out):
    N, D = x.shape
    E, DE = edge_attr.shape
    ROW = D + ROW_PAD
    ONE, SCORE = D, D + 1
    NCH = chunks_of(E)
    GROUPS = NCH // SLOTS
    H = D // P
    TP = max(p for p in range(1, P + 1) if N % p == 0)
    TABLE_GROUPS = table_groups(N // TP)
    BLOCKS = -(-N // P)
    WINDOWS = -(-N // WINDOW)
    NODE_COLS = BLOCKS * P + WINDOW
    SEL_EDGES = NCH * TILES
    assert D == 2 * P and DE == P and GROUPS >= 5 and NCH <= 512

    table = nc.dram_tensor("row_table", [N, ROW], F32, kind="Internal").ap()

    with ExitStack() as ctx:
        def sb(name, shape, dt=F32):
            return ctx.enter_context(nc.sbuf_tensor(name, shape, dt))

        def slots(stack, name, shape):
            return [stack.enter_context(nc.sbuf_tensor(f"{name}{s}", shape, F32)) for s in range(SLOTS)]

        def ps(name, shape):
            return ctx.enter_context(nc.psum_tensor(name, shape, F32))

        def sem(name):
            return ctx.enter_context(nc.semaphore(name))

        ident = sb("ident", [P, P])
        ones = sb("ones", [P, P])
        last_row = sb("last_row", [P, P])
        iota_sb = sb("iota_sb", [P, WINDOW])
        wn_sb = sb("wn_sb", [P, H, D])
        finish_w = sb("finish_w", [P, H + 1, D + 1])
        we_sb = sb("we_sb", [P, H, DE])
        cols = sb("cols", [P, 3, H])
        attn_wide = sb("attn_wide", [P, H, P])
        u_bc = sb("u_bc", [P, D])
        score_const = sb("score_const", [P, 2])
        dst_loc = sb("dst_loc", [P, SEL_EDGES])
        base_bc = sb("base_bc", [P, NCH])
        base_i = sb("base_i", [P, NCH], I32)
        src_idx = sb("src_idx", [P, SLOTS, TILES], I32)
        node_max = sb("node_max", [P, NODE_COLS])
        sums = sb("sums", [P, H + 1, NODE_COLS])
        tile_max = sb("tile_max", [P, P])
        node_sums = sb("node_sums", [P, (H + 1) * P])
        finished_below = sb("finished_below", [P, NCH])
        outside_i = sb("outside_i", [P, 1], I32)
        sums_here = slots(ctx, "sums_here", [P, H + 1, P])
        x_here = slots(ctx, "x_here", [P, D])
        gained = slots(ctx, "gained", [P, D])
        total = slots(ctx, "total", [P, 1])
        inverse = slots(ctx, "inverse", [P, 1])
        dst_left = sb("dst_left", [P, TILES])
        below_end = sb("below_end", [P, TILES])
        in_window = sb("in_window", [P, TILES])

        t_maxT = ps("t_maxT", [P, P])
        t_maxB = ps("t_maxB", [P, WINDOW])
        t_node = ps("t_node", [P, D + 1])
        t_sums = ps("t_sums", [P, H + 1, P])
        t_out = [ps(f"t_out{s}", [P, 512]) for s in range(SLOTS)]

        beside = ps("beside", [P, 512])
        v_bc = beside[:, 0:DE]
        node_iota = beside[:, DE:DE + WINDOW]
        new_max = beside[:, DE + WINDOW:DE + 2 * WINDOW]
        score = beside[:, DE + 2 * WINDOW:DE + 2 * WINDOW + TILES]

        t_setup = [t_out[0], t_out[1]]

        weights_in = sem("weights_in")
        dst_in = sem("dst_in")
        finish_w_in = sem("finish_w_in")
        consts_ready = sem("consts_ready")
        state_ready = sem("state_ready")
        src_in = [sem(f"src_in{s}") for s in range(SLOTS)]
        attr_in = [sem(f"attr_in{s}") for s in range(SLOTS)]
        rows_in = [sem(f"rows_in{s}") for s in range(SLOTS)]
        once = FinishSemaphores(sem, "once")
        again = FinishSemaphores(sem, "again")
        setup_step = sem("setup_step")
        attn_ready = sem("attn_ready")
        spread_ready = sem("spread_ready")
        vectors_ready = sem("vectors_ready")
        dst_float = sem("dst_float")
        base_spread = sem("base_spread")
        x_in = [sem(f"x_in{q}") for q in range(len(TABLE_GROUPS))]
        stats_ready = sem("stats_ready")
        aggregated = sem("aggregated")
        rstd_ready = sem("rstd_ready")
        var_ready = sem("var_ready")
        dev_ready = sem("dev_ready")
        shift_ready = sem("shift_ready")
        normed = sem("normed")
        row_ready = sem("row_ready")
        table_out = [sem(f"table_out{s}") for s in range(SLOTS)]
        attr_used = sem("attr_used")
        summed = sem("summed")
        scored = sem("scored")
        differs = sem("differs")
        masked_ready = sem("masked_ready")
        tile_max_ready = sem("tile_max_ready")
        maxT_ready = sem("maxT_ready")
        chunk_max_ready = sem("chunk_max_ready")
        diag_ready = sem("diag_ready")
        maxB_ready = sem("maxB_ready")
        new_max_ready = sem("new_max_ready")
        drop_ready = sem("drop_ready")
        max_stored = sem("max_stored")
        shifted = sem("shifted")
        decay_ready = sem("decay_ready")
        weights_ready = sem("weights_ready")
        multiplied = sem("multiplied")
        node_sums_ready = sem("node_sums_ready")
        sums_ready = sem("sums_ready")
        decayed = sem("decayed")
        sums_added = sem("sums_added")
        counted = sem("counted")
        count_spread = sem("count_spread")
        outside_ready = sem("outside_ready")
        left_step = sem("left_step")
        left_moved = sem("left_moved")
        passed = sem("passed")

        def stand(eng):
            eng.sem_inc(passed, 1)

        def per_tile(ap, t):
            return ap.unsqueeze(2).to_broadcast([P, TILES - t, WINDOW])

        def per_node(ap, t, end=TILES):
            return ap.unsqueeze(1).to_broadcast([P, end - t, WINDOW])

        def has(c, n):
            return not isinstance(c, int) or c >= n

        LAST = GROUPS - 1
        assert BLOCKS > LAST
        used = {0: (LAST - 3, LAST - 2)}

        def place(b, s):
            last_m, uses = used.get(s, (None, 0))
            used[s] = (b, uses + 1)
            return b, None if last_m is None else last_m + 1, s, uses, b, min(P, N - b * P)

        finish_in = {}
        first = LAST - 2
        for turn in (LAST - 1, LAST):
            even = turn * SLOTS * CHUNK * N // (E * P)
            count = max(1, min(SLOTS, even - first, BLOCKS - 1 - first))
            finish_in[turn] = [place(first + i, i) for i in range(count)]
            first += count
        behind_loop = [place(b, i % SLOTS) for i, b in enumerate(range(first, BLOCKS))]

        def in_turn(g):
            return g - 1, g - 1 if has(g, 2) else None, 0, g - 1, g - 1, P

        def each(step, eng, run, which):
            for block_of in which:
                step(eng, run, *block_of)

        def load_src(sp, c, s):
            sp.dma_start(src_idx[:, s, :], src_slots[bass.ds(c, 1), :, :].rearrange("o p j -> (o p) j")
                         ).then_inc(src_in[s], 16)

        with ExitStack() as st:
            x_rows = st.enter_context(nc.sbuf_tensor("x_rows", [TP, N // TP, D], F32))
            t_rows = [st.enter_context(nc.sbuf_tensor(f"t_rows{s}", [TP, GROUP_ROWS, ROW], F32)) for s in range(SLOTS)]
            stats = slots(st, "stats", [P, GROUP_ROWS, 6])
            mean_var = slots(st, "mean_var", [P, GROUP_ROWS, 2])
            var_eps = slots(st, "var_eps", [P, GROUP_ROWS])
            dev = slots(st, "dev", [P, GROUP_ROWS])
            rstd = slots(st, "rstd", [P, GROUP_ROWS])
            shift = slots(st, "shift", [P, GROUP_ROWS])

            def of_group(ap, q):
                first, count = TABLE_GROUPS[q]
                return ap.rearrange("(p r) c -> p r c", p=TP)[:, first:first + count, :]

            def group_rows(q):
                return range(TABLE_GROUPS[q][0], sum(TABLE_GROUPS[q])), range(TABLE_GROUPS[q][1])

            block = st.enter_context(nc.Block())

            @block.sync
            def _(sp):
                for q, (first, count) in enumerate(TABLE_GROUPS):
                    sp.dma_start(x_rows[:, first:first + count, :], of_group(x, q)).then_inc(x_in[q], 16)
                    if q == 0:
                        sp.dma_start(cols[:], vectors).then_inc(weights_in, 16)
                        sp.dma_start(wn_sb[:], Wn.rearrange("(h p) i -> p h i", p=P)).then_inc(weights_in, 16)
                        sp.dma_start(we_sb[:], We.rearrange("(h p) i -> p h i", p=P)).then_inc(weights_in, 16)
                for s in range(SLOTS):
                    load_src(sp, s, s)
                sp.wait_ge(state_ready, 1)
                sp.dma_start(finish_w[:, 0:H, 0:D], WnT.rearrange("(h p) o -> p h o", p=P)).then_inc(finish_w_in, 16)
                sp.dma_start(finish_w[0:1, H, 0:D], bn.rearrange("(a d) -> a d", a=1)).then_inc(finish_w_in, 16)

            @block.gpsimd
            def _(pool):
                nc.gpsimd.memset(ones[:], 1.0)
                nc.gpsimd.memset(ident[:], 0.0)
                nc.gpsimd.memset(last_row[:], 0.0)
                nc.gpsimd.memset(node_sums[:], 0.0)
                nc.gpsimd.memset(tile_max[:], 0.0)
                for s in range(SLOTS):
                    nc.gpsimd.memset(t_rows[s][:, :, D:ROW], 0.0)
                plain = (LAST - 1) * SLOTS
                nc.gpsimd.iota(finished_below[:, 0:plain], pattern=[[P, LAST - 1], [0, SLOTS]], base=0,
                               channel_multiplier=0, allow_small_or_imprecise_dtypes=True)
                for turn, blocks in finish_in.items():
                    nc.gpsimd.memset(finished_below[:, turn * SLOTS:(turn + 1) * SLOTS], float((blocks[-1][0] + 1) * P))
                nc.gpsimd.iota(iota_sb[:], pattern=[[1, WINDOW]], base=0, channel_multiplier=0,
                               allow_small_or_imprecise_dtypes=True)
                nc.gpsimd.memset(finish_w[:], 0.0).then_inc(state_ready, 1)
                pool.wait_ge(state_ready, 1)
                nc.gpsimd.affine_select(out=ident[:], in_=ident[:], compare_op=ALU.not_equal, fill=1.0,
                                        base=0, pattern=[[-1, P]], channel_multiplier=1)
                nc.gpsimd.affine_select(out=last_row[:], in_=last_row[:], compare_op=ALU.not_equal, fill=1.0,
                                        base=-(P - 1), pattern=[[0, P]], channel_multiplier=1)
                nc.gpsimd.affine_select(out=finish_w[:, H, D:D + 1], in_=finish_w[:, H, D:D + 1],
                                        compare_op=ALU.not_equal, fill=1.0,
                                        base=0, pattern=[[0, 1]], channel_multiplier=1)
                for s in range(SLOTS):
                    last = nc.gpsimd.memset(t_rows[s][:, :, ONE:ONE + 1], 1.0)
                last.then_inc(consts_ready, 1)
                nc.gpsimd.memset(node_max[:], NO_MAX)
                nc.gpsimd.memset(sums[:], 0.0).then_inc(state_ready, 1)

            @block.tensor
            def _(pe):
                pe.wait_ge(consts_ready, 1)
                pe.wait_ge(weights_in, 3 * 16)
                pe.wait_ge(attn_ready, 1)
                for h in range(H):
                    pe.matmul(t_setup[0][:, 0:D], attn_wide[:, h, :], wn_sb[:, h, :], start=(h == 0), stop=(h == H - 1))
                for h in range(H):
                    pe.matmul(t_setup[0][:, D:D + DE], attn_wide[:, h, :], we_sb[:, h, :], start=(h == 0), stop=(h == H - 1))
                for h in range(H):
                    mm = pe.matmul(t_setup[0][:, D + DE:D + DE + 2], attn_wide[:, h, :], cols[:, 1:3, h],
                                   start=(h == 0), stop=(h == H - 1))
                mm.then_inc(spread_ready, 1)

            def stats_of(dve, q):
                s = q % SLOTS
                dve.wait_ge(x_in[q], 16)
                for node, r in zip(*group_rows(q)):
                    last = nc.vector.bn_stats(stats[s][0:TP, r, :], x_rows[:, node, :])
                last.then_inc(stats_ready, 1)
                dve.wait_ge(stats_ready, q + 1)
                if q >= SLOTS:
                    dve.wait_ge(shift_ready, q - SLOTS + 1)
                    dve.wait_ge(dev_ready, q - SLOTS + 1)
                for r in range(TABLE_GROUPS[q][1]):
                    last = nc.vector.bn_aggr(mean_var[s][0:TP, r, :], stats[s][0:TP, r, :])
                last.then_inc(aggregated, 1)
                dve.wait_ge(aggregated, q + 1)
                here = slice(0, TABLE_GROUPS[q][1])
                nc.vector.tensor_scalar(var_eps[s][0:TP, here], mean_var[s][0:TP, here, 1], LN_EPS, None, ALU.add
                                        ).then_inc(var_ready, 1)

            def shift_of(dve, q):
                s = q % SLOTS
                here = slice(0, TABLE_GROUPS[q][1])
                dve.wait_ge(dev_ready, q + 1)
                if q >= SLOTS:
                    dve.wait_ge(normed, q - SLOTS + 1)
                nc.vector.reciprocal(rstd[s][0:TP, here], dev[s][0:TP, here]).then_inc(rstd_ready, 1)
                dve.wait_ge(rstd_ready, q + 1)
                nc.vector.scalar_tensor_tensor(shift[s][0:TP, here], mean_var[s][0:TP, here, 0], -1.0,
                                               rstd[s][0:TP, here], ALU.mult, ALU.mult).then_inc(shift_ready, 1)

            def node_scores(dve, q):
                s = q % SLOTS
                dve.wait_ge(normed, q + 1)
                for node, r in zip(*group_rows(q)):
                    last = nc.vector.tensor_tensor_reduce(x_rows[:, node, :], t_rows[s][:, r, 0:D], u_bc[0:TP, :], 1.0,
                                                          score_const[0:TP, 0:1], ALU.mult, ALU.add,
                                                          t_rows[s][:, r, SCORE:SCORE + 1])
                last.then_inc(row_ready, 1)

            @block.vector
            def _(dve):
                stats_of(dve, 0)
                dve.wait_ge(consts_ready, 1)
                dve.wait_ge(weights_in, 3 * 16)
                for h in range(H):
                    last = nc.vector.tensor_scalar(attn_wide[:, h, :], ones[:], cols[:, 0, h:h + 1], None, ALU.mult)
                last.then_inc(attn_ready, 1)
                shift_of(dve, 0)
                if len(TABLE_GROUPS) > 1:
                    stats_of(dve, 1)
                dve.wait_ge(spread_ready, 1)
                nc.vector.tensor_copy(u_bc[:], t_setup[0][:, 0:D])
                nc.vector.tensor_copy(node_iota, iota_sb[:])
                nc.vector.tensor_copy(v_bc, t_setup[0][:, D:D + DE])
                nc.vector.tensor_copy(score_const[:], t_setup[0][:, D + DE:D + DE + 2]).then_inc(setup_step, 1)
                dve.wait_ge(setup_step, 1)
                nc.vector.tensor_tensor(score_const[:, 0:1], score_const[:, 0:1], score_const[:, 1:2],
                                        ALU.add).then_inc(vectors_ready, 1)
                dve.wait_ge(vectors_ready, 1)
                for q in range(len(TABLE_GROUPS)):
                    if q + 1 < len(TABLE_GROUPS):
                        shift_of(dve, q + 1)
                    if q + 2 < len(TABLE_GROUPS):
                        stats_of(dve, q + 2)
                    node_scores(dve, q)

            @block.scalar
            def _(act):
                def deviation(q):
                    s = q % SLOTS
                    here = slice(0, TABLE_GROUPS[q][1])
                    act.wait_ge(var_ready, q + 1)
                    if q >= SLOTS:
                        act.wait_ge(rstd_ready, q - SLOTS + 1)
                    nc.scalar.activation(dev[s][0:TP, here], var_eps[s][0:TP, here], ACT.Sqrt).then_inc(dev_ready, 1)

                def store_rows(q):
                    act.wait_ge(row_ready, q + 1)
                    act.dma_start(of_group(table, q), t_rows[q % SLOTS][:, 0:TABLE_GROUPS[q][1], :]
                                  ).then_inc(table_out[q % SLOTS], 16)

                deviation(0)
                if len(TABLE_GROUPS) > 1:
                    deviation(1)
                act.wait_ge(consts_ready, 1)
                for q in range(len(TABLE_GROUPS)):
                    s = q % SLOTS
                    act.wait_ge(shift_ready, q + 1)
                    if q >= SLOTS:
                        act.wait_ge(table_out[s], 16 * (q // SLOTS))
                    for node, r in zip(*group_rows(q)):
                        last = nc.scalar.activation(t_rows[s][:, r, 0:D], x_rows[:, node, :], ACT.Relu,
                                                    bias=shift[s][0:TP, r:r + 1], scale=rstd[s][0:TP, r:r + 1])
                    last.then_inc(normed, 1)
                    if q + 2 < len(TABLE_GROUPS):
                        deviation(q + 2)
                    if q >= 1:
                        store_rows(q - 1)
                store_rows(len(TABLE_GROUPS) - 1)
                for s in range(SLOTS):
                    act.wait_ge(table_out[s], 16 * len(range(s, len(TABLE_GROUPS), SLOTS)))

        chunk_stack = ctx.enter_context(ExitStack())

        def chunk_sb(name, shape, dt=F32):
            return chunk_stack.enter_context(nc.sbuf_tensor(name, shape, dt))

        rows = chunk_sb("rows", [P, SLOTS, TILES, ROW])
        attr = chunk_sb("attr", [P, SLOTS, TILES, DE])
        attr_dot = chunk_sb("attr_dot", [P, TILES])
        score_sum = chunk_sb("score_sum", [P, TILES])
        masked = chunk_sb("masked", [P, TILES, WINDOW])
        weights = chunk_sb("weights", [P, SLOTS, TILES, WINDOW])
        chunk_max = chunk_sb("chunk_max", [WINDOW, 1])
        max_diag = chunk_sb("max_diag", [WINDOW, WINDOW])
        decay = chunk_sb("decay", [P, SLOTS, WINDOW])
        max_drop = chunk_sb("max_drop", [P, SLOTS, WINDOW])
        dst_i = chunk_sb("dst_i", [P, SEL_EDGES], I32)
        in_flag = dst_i[:].bitcast(F32)
        in_count = chunk_sb("in_count", [P, 1])

        def rows_at(ap, b, n):
            return ap[b * P:b * P + n, :] if isinstance(b, int) else ap[bass.ds(b * P, n), :]

        def load_x(eng, f, m, before, s, turn, b, n):
            if before is not None:
                eng.wait_ge(f.added, before)
                stand(eng)
            eng.dma_start(x_here[s][0:n, :], rows_at(x, b, n)).then_inc(f.x_in[s], 16)

        def take_sums(dve, f, m, before, s, turn, b, n):
            if before is not None:
                dve.wait_ge(f.projected, before)
                stand(dve)
            nc.vector.tensor_copy(sums_here[s][:], sums[:, :, bass.ds(b * P, P)]).then_inc(f.taken, 1)

        def project(pe, f, m, before, s, turn, b, n):
            pe.wait_ge(f.taken, m + 1)
            if before is not None:
                pe.wait_ge(f.averaged, before)
            for h in range(H + 1):
                mm = pe.matmul(t_out[s][:, 0:D + 1], sums_here[s][:, h, :], finish_w[:, h, :],
                               start=(h == 0), stop=(h == H))
            mm.then_inc(f.projected, 1)

        def invert(dve, f, m, before, s, turn, b, n):
            dve.wait_ge(f.projected, m + 1)
            if before is not None:
                dve.wait_ge(f.averaged, before)
            nc.vector.tensor_scalar(total[s][:], t_out[s][:, D:D + 1], DENOM_EPS, None, ALU.add).then_inc(f.totalled, 1)
            dve.wait_ge(f.totalled, m + 1)
            nc.vector.reciprocal(inverse[s][:], total[s][:]).then_inc(f.inverted, 1)

        def average(act, f, m, before, s, turn, b, n):
            act.wait_ge(f.inverted, m + 1)
            if before is not None:
                act.wait_ge(f.stored[s], 16 * turn)
            nc.scalar.activation(gained[s][:], t_out[s][:, 0:D], ACT.Relu, scale=inverse[s][:, 0:1]).then_inc(f.averaged, 1)

        def add_x(eng, f, m, before, s, turn, b, n):
            eng.wait_ge(f.averaged, m + 1)
            eng.wait_ge(f.x_in[s], 16 * (turn + 1))
            eng.tensor_tensor(gained[s][0:n, :], gained[s][0:n, :], x_here[s][0:n, :], ALU.add).then_inc(f.added, 1)

        def store(eng, f, m, before, s, turn, b, n):
            eng.wait_ge(f.added, m + 1)
            eng.dma_start(rows_at(out, b, n), gained[s][0:n, :]).then_inc(f.stored[s], 16)

        def dot_attr(dve, s, landed, tiles):
            dve.wait_ge(attr_in[s], landed)
            for j in tiles:
                last = nc.vector.tensor_tensor_reduce(attr[:, s, j, :], attr[:, s, j, :], v_bc, 1.0, 0.0,
                                                      ALU.mult, ALU.add, attr_dot[:, j:j + 1])
            if tiles[-1] == TILES - 1:
                last.then_inc(attr_used, 1)

        def add_scores(dve, s, c, landed, t):
            dve.wait_ge(rows_in[s], landed)
            dve.wait_ge(attr_used, c + 1)
            nc.vector.tensor_tensor(score_sum[:, t:], attr_dot[:, t:], rows[:, s, t:, SCORE], ALU.add).then_inc(summed, 1)
            dve.wait_ge(summed, c + 1)
            nc.vector.scalar_tensor_tensor(score[:, t:], score_sum[:, t:], NEG_SLOPE, score_sum[:, t:],
                                           ALU.mult, ALU.max).then_inc(scored, 1)

        def compare(dve, dst_here, t):
            nc.vector.tensor_tensor(masked[:, t:, :], per_node(node_iota, t), per_tile(dst_here, t),
                                    ALU.not_equal).then_inc(differs, 1)

        def mask(dve, c, chunks, t):
            dve.wait_ge(differs, c + 1)
            dve.wait_ge(scored, chunks + 1)
            nc.vector.scalar_tensor_tensor(masked[:, t:, :], masked[:, t:, :], MASKED, per_tile(score[:, t:], t),
                                           ALU.mult, ALU.add).then_inc(masked_ready, 1)
            dve.wait_ge(masked_ready, c + 1)
            if has(c, 1):
                dve.wait_ge(maxT_ready, c)
            nc.vector.tensor_reduce(tile_max[:, 0:WINDOW], masked[:, t:, :].rearrange("p j n -> p n j"),
                                    AX.X, ALU.max).then_inc(tile_max_ready, 1)

        def chunk_maximum(dve, c):
            dve.wait_ge(maxT_ready, c + 1)
            nc.vector.tensor_reduce(chunk_max[:], t_maxT[0:WINDOW, :], AX.X, ALU.max).then_inc(chunk_max_ready, 1)
            dve.wait_ge(chunk_max_ready, c + 1)
            if has(c, 1):
                dve.wait_ge(maxB_ready, c)
            nc.vector.tensor_scalar(max_diag[:], ident[0:WINDOW, 0:WINDOW], chunk_max[:, 0:1], None,
                                    ALU.mult).then_inc(diag_ready, 1)

        def halves(t):
            mid = (t + TILES) // 2
            return slice(t, mid), slice(mid, TILES)

        def grow_maximum(dve, c, s, first_node, t):
            here = node_max[:, bass.ds(first_node, WINDOW)]
            dve.wait_ge(maxB_ready, c + 1)
            nc.vector.tensor_tensor(new_max, here, t_maxB[:], ALU.max).then_inc(new_max_ready, 1)
            dve.wait_ge(new_max_ready, c + 1)
            for part in halves(t):
                nc.vector.tensor_tensor(masked[:, part, :], masked[:, part, :],
                                        per_node(new_max, part.start, part.stop), ALU.subtract).then_inc(shifted, 1)
            if has(c, SLOTS):
                dve.wait_ge(decay_ready, c - SLOTS + 1)
            nc.vector.tensor_tensor(max_drop[:, s, :], here, new_max, ALU.subtract).then_inc(drop_ready, 1)
            dve.wait_ge(drop_ready, c + 1)
            nc.vector.tensor_tensor(here, here, new_max, ALU.max).then_inc(max_stored, 1)

        def add_sums(dve, c, s, first_node):
            here = sums[:, :, bass.ds(first_node, WINDOW)]
            dve.wait_ge(decay_ready, c + 1)
            if has(c, 1):
                dve.wait_ge(sums_added, c)
            nc.vector.tensor_tensor(here, here, decay[:, s, :].unsqueeze(1).to_broadcast([P, H + 1, WINDOW]),
                                    ALU.mult).then_inc(decayed, 1)
            dve.wait_ge(decayed, c + 1)
            dve.wait_ge(sums_ready, c + 1)
            nc.vector.tensor_tensor(here, here, t_sums[:, :, 0:WINDOW], ALU.add).then_inc(sums_added, 1)

        def turn_maxima(pe, c):
            pe.wait_ge(tile_max_ready, c + 1)
            if has(c, 1):
                pe.wait_ge(chunk_max_ready, c)
            pe.transpose(t_maxT[:], tile_max[:], ident[:]).then_inc(maxT_ready, 1)

        def spread_maxima(pe, c):
            pe.wait_ge(diag_ready, c + 1)
            if has(c, 1):
                pe.wait_ge(new_max_ready, c)
            pe.matmul(t_maxB[:], ones[0:WINDOW, :], max_diag[:], start=True, stop=True).then_inc(maxB_ready, 1)

        def multiply(pe, c, s, t):
            for half, part in enumerate(halves(t)):
                pe.wait_ge(weights_ready, 2 * c + half + 1)
                for j in range(part.start, part.stop):
                    mm = pe.matmul(t_node[0:WINDOW, :], weights[:, s, j, :], rows[:, s, j, 0:D + 1],
                                   start=(j == t), stop=(j == TILES - 1))
            mm.then_inc(multiplied, 1)

        def turn_sums(pe, c):
            pe.wait_ge(node_sums_ready, c + 1)
            if has(c, 1):
                pe.wait_ge(sums_added, c)
            for h in range(H + 1):
                mm = pe.transpose(t_sums[:, h, :], node_sums[:, h * P:(h + 1) * P], ident[:])
            mm.then_inc(sums_ready, 1)

        def exponentials(act, c, s, t):
            if has(c, SLOTS):
                act.wait_ge(multiplied, c - SLOTS + 1)
                stand(act)
            for half, part in enumerate(halves(t)):
                act.wait_ge(shifted, 2 * c + half + 1)
                nc.scalar.activation(weights[:, s, part, :], masked[:, part, :], ACT.Exp).then_inc(weights_ready, 1)
            act.wait_ge(drop_ready, c + 1)
            if has(c, SLOTS):
                act.wait_ge(decayed, c - SLOTS + 1)
            nc.scalar.activation(decay[:, s, :], max_drop[:, s, :], ACT.Exp).then_inc(decay_ready, 1)

        def copy_sums(act, c):
            act.wait_ge(multiplied, c + 1)
            if has(c, 1):
                act.wait_ge(sums_ready, c)
            nc.scalar.copy(node_sums[0:WINDOW, 0:D], t_node[0:WINDOW, 0:D])
            nc.scalar.copy(node_sums[0:WINDOW, D:D + P], t_node[0:WINDOW, D:D + 1].to_broadcast([WINDOW, P])
                           ).then_inc(node_sums_ready, 1)

        with ExitStack() as st:
            block = st.enter_context(nc.Block())
            last_turn = [(LAST * SLOTS + s, first_tile(LAST * SLOTS + s, E)) for s in range(SLOTS)]
            TURN_ROWS = 16 * TILES

            def rows_landed(c, g, s):
                if isinstance(c, int) and c >= LAST * SLOTS:
                    return TURN_ROWS * g + 16 * (TILES - first_tile(c, E))
                return TURN_ROWS * (g + 1)

            @block.sync
            def _(sp):
                def load(c, g, s, t=0, edges=None):
                    if has(c, SLOTS):
                        sp.wait_ge(rows_in[s], TURN_ROWS * g)
                        stand(sp)
                        sp.wait_ge(attr_used, c - SLOTS + 1)
                        stand(sp)
                        load_src(sp, c, s)
                    if edges is None:
                        edges = edge_attr[bass.ds(c * CHUNK, CHUNK), :]
                    sp.dma_start(attr[:, s, t:, :], edges.rearrange("(p j) k -> p j k", p=P)).then_inc(attr_in[s], 16)

                sp.dma_start(dst_i[:], dst_slots).then_inc(dst_in, 16)
                for s in range(SLOTS):
                    load(s, 0, s)
                with sp.Fori(1, LAST) as g:
                    for s in range(SLOTS):
                        load(g * SLOTS + s, g, s)
                for s, (c, t) in enumerate(last_turn):
                    at = chunk_start(c, E)
                    load(c, LAST, s, t, edge_attr[at:at + (TILES - t) * P, :])
                each(store, sp, once, finish_in[LAST])
                each(store, sp, once, behind_loop)

            @block.gpsimd
            def _(pool):
                def gather(c, g, s, t=0):
                    pool.wait_ge(src_in[s], 16 * (g + 1))
                    if has(c, SLOTS):
                        pool.wait_ge(multiplied, c - SLOTS + 1)
                    stand(pool)
                    for j in range(t, TILES):
                        pool.indirect_dma_start(rows[:, s, j, :], None, table,
                                                bass.IndirectOffsetOnAxis(ap=src_idx[:, s, j:j + 1], axis=0)
                                                ).then_inc(rows_in[s], 16)

                for s in range(SLOTS):
                    gather(s, 0, s)
                with pool.Fori(1, LAST) as g:
                    for s in range(SLOTS):
                        gather(g * SLOTS + s, g, s)
                for s, (c, t) in enumerate(last_turn):
                    gather(c, LAST, s, t)

            @block.vector
            def _(dve):
                def chunk(c, g, s, t=0, finishing=(), next_t=0):
                    def dot_part(i):
                        if next_t is None:
                            return
                        n = TILES - next_t
                        tiles = range(next_t + i * n // 3, next_t + (i + 1) * n // 3)
                        dot_attr(dve, (s + 1) % SLOTS, 16 * (g + (s + 1) // SLOTS + 1), tiles)

                    if has(c, 1):
                        dve.wait_ge(weights_ready, 2 * c)
                    compare(dve, dst_loc[:, bass.ds(c * TILES + t, TILES - t)], t)
                    add_scores(dve, s, c, rows_landed(c, g, s), t)
                    mask(dve, c, c, t)
                    dot_part(0)
                    if s == 1:
                        each(invert, dve, once, finishing)
                    chunk_maximum(dve, c)
                    dot_part(1)
                    here = dve.value_load(base_i[0:1, bass.ds(c, 1)], min_val=0, max_val=N - 1)
                    grow_maximum(dve, c, s, here, t)
                    if has(c, 1):
                        before = dve.value_load(base_i[0:1, bass.ds(c - 1, 1)], min_val=0, max_val=N - 1)
                        add_sums(dve, c - 1, (s - 1) % SLOTS, before)
                    if s == 0 and finishing:
                        dve.wait_ge(sums_added, c)
                        each(take_sums, dve, once, finishing)
                    dot_part(2)
                    if s == 2:
                        each(add_x, dve, once, finishing)
                    dve.wait_ge(max_stored, c + 1)
                    stand(dve)

                dve.wait_ge(dst_in, 16)
                nc.vector.tensor_copy(dst_loc[:], dst_i[:]).then_inc(dst_float, 1)
                dve.wait_ge(base_spread, 1)
                nc.vector.tensor_scalar(base_bc[:], t_setup[1][:, 0:NCH], float(WINDOW - 1), 0.0,
                                        ALU.subtract, ALU.max).then_inc(setup_step, 1)
                dve.wait_ge(setup_step, 2)
                nc.vector.tensor_copy(base_i[:], base_bc[:])
                dst_by_chunk = dst_loc[:].rearrange("p (c j) -> p c j", j=TILES)
                nc.vector.tensor_tensor(dst_by_chunk, dst_by_chunk,
                                        base_bc[:].unsqueeze(2).to_broadcast([P, NCH, TILES]),
                                        ALU.subtract).then_inc(setup_step, 1)
                dve.wait_ge(setup_step, 3)
                dot_attr(dve, 0, 16, range(TILES))
                for s in range(SLOTS):
                    chunk(s, 0, s)
                nc.vector.tensor_tensor(finished_below[:], finished_below[:], base_bc[:], ALU.subtract).then_inc(counted, 1)
                dve.wait_ge(counted, 1)
                nc.vector.tensor_scalar(finished_below[:], finished_below[:], 0.0, None, ALU.max).then_inc(counted, 1)
                dve.wait_ge(counted, 2)
                nc.vector.tensor_tensor(in_flag.rearrange("p (c j) -> p c j", j=TILES), dst_by_chunk,
                                        finished_below[:].unsqueeze(2).to_broadcast([P, NCH, TILES]),
                                        ALU.is_ge).then_inc(counted, 1)
                dve.wait_ge(counted, 3)
                nc.vector.scalar_tensor_tensor(in_flag, dst_loc[:], WINDOW - 0.5, in_flag, ALU.is_lt, ALU.mult
                                               ).then_inc(counted, 1)
                dve.wait_ge(counted, 4)
                nc.vector.tensor_reduce(in_count[:], in_flag, AX.X, ALU.add).then_inc(counted, 1)
                for s in range(SLOTS):
                    chunk(SLOTS + s, 1, s, finishing=[in_turn(1)])
                dve.wait_ge(count_spread, 1)
                nc.vector.tensor_scalar(outside_i[:], t_setup[1][:, 0:1], -1.0, float(E), ALU.mult, ALU.add
                                        ).then_inc(outside_ready, 1)
                with dve.Fori(2, LAST - 1) as g:
                    for s in range(SLOTS):
                        chunk(g * SLOTS + s, g, s, finishing=[in_turn(g)])
                for s in range(SLOTS):
                    last_next = first_tile(LAST * SLOTS, E) if s == SLOTS - 1 else 0
                    chunk((LAST - 1) * SLOTS + s, LAST - 1, s, finishing=finish_in[LAST - 1], next_t=last_next)
                for s, (c, t) in enumerate(last_turn):
                    chunk(c, LAST, s, t, finishing=finish_in[LAST],
                          next_t=last_turn[s + 1][1] if s + 1 < SLOTS else None)
                end = dve.value_load(base_i[0:1, NCH - 1:NCH], min_val=0, max_val=N - 1)
                add_sums(dve, NCH - 1, SLOTS - 1, end)
                dve.wait_ge(sums_added, NCH)
                for i in range(len(behind_loop) + 2):
                    each(take_sums, dve, once, behind_loop[i:i + 1])
                    each(invert, dve, once, behind_loop[max(0, i - 1):i])
                    each(add_x, dve, once, behind_loop[max(0, i - 2):max(0, i - 1)])
                dve.wait_ge(outside_ready, 1)

            @block.tensor
            def _(pe):
                def chunk(c, s, t=0, finishing=()):
                    if s == 1:
                        each(project, pe, once, finishing)
                    turn_maxima(pe, c)
                    if has(c, 1):
                        turn_sums(pe, c - 1)
                    spread_maxima(pe, c)
                    multiply(pe, c, s, t)

                pe.wait_ge(dst_float, 1)
                pe.matmul(t_setup[1][:, 0:NCH], last_row[:],
                          dst_loc[:].rearrange("p (c j) -> p c j", j=TILES)[:, :, TILES - 1],
                          start=True, stop=True).then_inc(base_spread, 1)
                for s in range(SLOTS):
                    chunk(s, s)
                pe.wait_ge(counted, 5)
                pe.matmul(t_setup[1][:, 0:1], ones[:], in_count[:], start=True, stop=True).then_inc(count_spread, 1)
                pe.wait_ge(finish_w_in, 2 * 16)
                for s in range(SLOTS):
                    chunk(SLOTS + s, s, finishing=[in_turn(1)])
                with pe.Fori(2, LAST - 1) as g:
                    for s in range(SLOTS):
                        chunk(g * SLOTS + s, s, finishing=[in_turn(g)])
                for s in range(SLOTS):
                    chunk((LAST - 1) * SLOTS + s, s, finishing=finish_in[LAST - 1])
                pe.wait_ge(outside_ready, 1)
                for s, (c, t) in enumerate(last_turn):
                    chunk(c, s, t, finishing=finish_in[LAST])
                turn_sums(pe, NCH - 1)
                each(project, pe, once, behind_loop)

            @block.scalar
            def _(act):
                def chunk(c, s, t=0):
                    exponentials(act, c, s, t)
                    copy_sums(act, c)

                def finish_of(g):
                    if isinstance(g, int) and g in finish_in:
                        return finish_in[g]
                    return [in_turn(g)] if has(g, 1) else []

                def turn(g, chunks):
                    for s, (c, t) in enumerate(chunks):
                        exponentials(act, c, s, t)
                        if s == 1:
                            each(average, act, once, finish_of(g))
                        copy_sums(act, c)
                        if s == 0:
                            if has(g, 2):
                                each(store, act, once, finish_of(g - 1))
                            each(load_x, act, once, finish_of(g))

                def whole(g):
                    return [(g * SLOTS + s, 0) for s in range(SLOTS)]

                turn(0, whole(0))
                turn(1, whole(1))
                with act.Fori(2, LAST - 1) as g:
                    turn(g, whole(g))
                turn(LAST - 1, whole(LAST - 1))
                turn(LAST, last_turn)
                for i in range(len(behind_loop) + 2):
                    each(load_x, act, once, behind_loop[i:i + 1])
                    each(average, act, once, behind_loop[max(0, i - 2):max(0, i - 1)])

        with ExitStack() as st:
            block = st.enter_context(nc.Block())

            def if_outside(eng):
                outside = eng.value_load(outside_i[0:1, 0:1], min_val=0, max_val=E)
                return eng.If(outside > 0)

            rows_before = rows_landed(LAST * SLOTS, LAST, 0)

            def again_blocks(*steps):
                whole = (BLOCKS - 1) // SLOTS

                def do(m, before, s, turn, n):
                    for step, eng in steps:
                        step(eng, again, m, before, s, turn, m, n)

                eng = steps[0][1]
                for s in range(SLOTS):
                    do(s, None, s, 0, P)
                with eng.Fori(1, whole) as g:
                    for s in range(SLOTS):
                        do(g * SLOTS + s, (g - 1) * SLOTS + s + 1, s, g, P)
                for m in range(whole * SLOTS, BLOCKS):
                    do(m, m - SLOTS + 1, m % SLOTS, m // SLOTS, min(P, N - m * P))
                stand(eng)

            @block.sync
            def _(sp):
                for s in range(SLOTS):
                    if s in used:
                        sp.wait_ge(once.stored[s], 16 * used[s][1])
                with if_outside(sp):
                    def load(c, t, edges):
                        sp.wait_ge(rows_in[0], rows_before + TURN_ROWS * c)
                        stand(sp)
                        sp.wait_ge(attr_used, NCH + c)
                        stand(sp)
                        load_src(sp, c, 0)
                        sp.dma_start(attr[:, 0, t:, :], edges.rearrange("(p j) k -> p j k", p=P)).then_inc(attr_in[0], 16)

                    with sp.Fori(0, LAST * SLOTS) as c:
                        load(c, 0, edge_attr[bass.ds(c * CHUNK, CHUNK), :])
                    for c, t in last_turn:
                        at = chunk_start(c, E)
                        load(c, t, edge_attr[at:at + (TILES - t) * P, :])
                    again_blocks((store, sp))
                    for s in range(SLOTS):
                        sp.wait_ge(again.stored[s], 16 * len(range(s, BLOCKS, SLOTS)))
                    stand(sp)

            @block.gpsimd
            def _(pool):
                with if_outside(pool):
                    with pool.Fori(0, NCH) as c:
                        pool.wait_ge(src_in[0], 16 * (GROUPS + c + 1))
                        pool.wait_ge(multiplied, NCH + c * WINDOWS)
                        stand(pool)
                        for j in range(TILES):
                            pool.indirect_dma_start(rows[:, 0, j, :], None, table,
                                                    bass.IndirectOffsetOnAxis(ap=src_idx[:, 0, j:j + 1], axis=0)
                                                    ).then_inc(rows_in[0], 16)
                    again_blocks((add_x, pool))

            @block.vector
            def _(dve):
                with if_outside(dve):
                    with dve.Fori(0, NCH) as c:
                        dot_attr(dve, 0, 16 * (GROUPS + c + 1), range(TILES))
                        add_scores(dve, 0, NCH + c, rows_before + TURN_ROWS * (c + 1), 0)
                        dst_here = dst_loc[:, bass.ds(c * TILES, TILES)]
                        nc.vector.tensor_scalar(below_end[:], dst_here, WINDOW - 0.5, None, ALU.is_lt).then_inc(left_step, 1)
                        nc.vector.tensor_tensor(dst_left[:], dst_here,
                                                base_bc[:, bass.ds(c, 1)].to_broadcast([P, TILES]), ALU.add)
                        dve.wait_ge(left_step, 3 * c + 1)
                        nc.vector.scalar_tensor_tensor(in_window[:], dst_here, -0.5, below_end[:], ALU.is_gt, ALU.mult
                                                       ).then_inc(left_step, 1)
                        dve.wait_ge(left_step, 3 * c + 2)
                        nc.vector.scalar_tensor_tensor(dst_left[:], in_window[:], -float(1 << 20), dst_left[:],
                                                       ALU.mult, ALU.add).then_inc(left_step, 1)
                        dve.wait_ge(left_step, 3 * c + 3)
                        stand(dve)
                        with dve.Fori(0, WINDOWS) as w:
                            n = NCH + c * WINDOWS + w
                            compare(dve, dst_left[:], 0)
                            dve.wait_ge(differs, n + 1)
                            nc.vector.tensor_scalar(dst_left[:], dst_left[:], float(WINDOW), None, ALU.subtract
                                                    ).then_inc(left_moved, 1)
                            mask(dve, n, NCH + c, 0)
                            chunk_maximum(dve, n)
                            grow_maximum(dve, n, 0, w * WINDOW, 0)
                            add_sums(dve, n, 0, w * WINDOW)
                            dve.wait_ge(sums_added, n + 1)
                            dve.wait_ge(left_moved, c * WINDOWS + w + 1)
                            stand(dve)
                    again_blocks((take_sums, dve), (invert, dve))

            @block.tensor
            def _(pe):
                with if_outside(pe):
                    with pe.Fori(0, NCH) as c:
                        with pe.Fori(0, WINDOWS) as w:
                            n = NCH + c * WINDOWS + w
                            turn_maxima(pe, n)
                            spread_maxima(pe, n)
                            multiply(pe, n, 0, 0)
                            turn_sums(pe, n)
                    again_blocks((project, pe))

            @block.scalar
            def _(act):
                with if_outside(act):
                    with act.Fori(0, NCH) as c:
                        with act.Fori(0, WINDOWS) as w:
                            n = NCH + c * WINDOWS + w
                            exponentials(act, n, 0, 0)
                            copy_sums(act, n)
                    for s in range(SLOTS):
                        if s in used:
                            act.wait_ge(once.stored[s], 16 * used[s][1])
                    again_blocks((load_x, act), (average, act))
    return nc


def layout(src, dst):
    import numpy as np
    E = src.shape[0]
    n = chunks_of(E)
    src_slots = np.zeros((n, P, TILES), src.dtype)
    dst_slots = np.full((n, P, TILES), -1, dst.dtype)
    for c in range(n):
        t = first_tile(c, E)
        edge = chunk_start(c, E) + np.arange(P)[:, None] * (TILES - t) + np.arange(TILES - t)
        src_slots[c, :, t:] = src[edge]
        dst_slots[c, :, t:] = np.where(edge < c * CHUNK, -1, dst[edge])
    return src_slots, np.ascontiguousarray(dst_slots.transpose(1, 0, 2).reshape(P, n * TILES))


def kernel(x, src, dst, edge_attr_128, L0_gnn_Wn, L0_gnn_bn, L0_gnn_We, L0_gnn_be, L0_gnn_attn):
    import numpy as np
    from concourse import bacc
    from concourse.bass_utils import run_bass_kernel_spmd

    src_slots, dst_slots = layout(np.asarray(src), np.asarray(dst))
    vectors = np.stack([np.asarray(v).reshape(-1, P).T for v in (L0_gnn_attn, L0_gnn_bn, L0_gnn_be)], axis=1)
    arrays = {
        "x": x, "src_slots": src_slots, "dst_slots": dst_slots, "edge_attr": edge_attr_128,
        "Wn": L0_gnn_Wn, "WnT": np.ascontiguousarray(np.asarray(L0_gnn_Wn).T), "We": L0_gnn_We,
        "bn": L0_gnn_bn, "vectors": vectors,
    }
    arrays = {k: np.ascontiguousarray(a) for k, a in arrays.items()}
    nc = bacc.Bacc("TRN2", target_bir_lowering=False, num_devices=1)
    aps = [nc.dram_tensor(f"in_{k}", a.shape, mybir.dt.from_np(a.dtype), kind="ExternalInput").ap()
           for k, a in arrays.items()]
    out = nc.dram_tensor("out", arrays["x"].shape, F32, kind="ExternalOutput").ap()
    gnn_layer(nc, *aps, out)
    r = run_bass_kernel_spmd(nc, [{f"in_{k}": a for k, a in arrays.items()}], core_ids=[0])
    return r.results[0]["out"]
```
